# Optimizing a Trainium2 kernel written in Bass

```python
import numpy as np
import jax
import jax.numpy as jnp

def _softmax(x, axis=-1):
    return jax.nn.softmax(x, axis=axis)

def _gelu(x):
    return jax.nn.gelu(x, approximate=True)

def _silu(x):
    return jax.nn.silu(x)

def _sigmoid(x):
    return jax.nn.sigmoid(x)

def _layernorm(x, axis=-1, eps=1e-05):
    m = jnp.mean(x, axis=axis, keepdims=True)
    v = jnp.var(x, axis=axis, keepdims=True)
    return (x - m) / jnp.sqrt(v + eps)

def _scatter_add(tgt, idx, src, axis=0):
    return tgt.at[idx].add(src)

def _segment_sum(src, seg, n):
    return jax.ops.segment_sum(src, seg, n)
kernel_name = 'mk_lm_tower_d1_tok_ids1024_r4_bceca1'

def setup_inputs(seed: int=0):
    np.random.seed(seed)
    _w = jnp.asarray

    def _rec_inputs():
        import jax
        import jax.numpy as jnp
        _rk = jax.random.key(seed)
        x = jax.random.randint(jax.random.fold_in(_rk, 1), (16, 256), 0, 12564, jnp.int32)
        return x
    x = _rec_inputs()

    def _L0_tok_setup():
        import jax, jax.numpy as jnp
        import numpy as np
        VOCAB = 50257
        HIDDEN = 256
        key = jax.random.key(seed)
        k1, k2, k3 = jax.random.split(key, 3)
        seq = jax.random.randint(k1, (8, 1024), 0, VOCAB, dtype=jnp.int64 if jax.config.jax_enable_x64 else jnp.int32)
        bound = 1.0 / np.sqrt(VOCAB)
        W = jax.random.uniform(k2, (HIDDEN, VOCAB), jnp.float32, -bound, bound)
        b = jax.random.uniform(k3, (HIDDEN,), jnp.float32, -bound, bound)
        return {'seq': seq, 'W': W, 'b': b}
    _L0_tok_all = _L0_tok_setup()
    _L0_tok_in = {k: v for k, v in _L0_tok_all.items() if k in ('W', 'b')}
    del _L0_tok_all

    def _L0_attn_setup():
        import jax, jax.numpy as jnp
        import numpy as np
        NUM_HEADS = 16
        key = jax.random.key(seed)
        k1, k2, k3 = jax.random.split(key, 3)
        S, B, E = (512, 4, 256)
        std = float(np.sqrt(2.0 / (E + E)))
        query = jax.random.normal(k1, (S, B, E), dtype=jnp.float32)
        in_proj_weight = jax.random.normal(k2, (3 * E, E), dtype=jnp.float32) * std
        in_proj_bias = jnp.zeros((3 * E,), dtype=jnp.float32)
        out_proj_weight = jax.random.normal(k3, (E, E), dtype=jnp.float32) * std
        out_proj_bias = jnp.zeros((E,), dtype=jnp.float32)
        return {'query': query, 'in_proj_weight': in_proj_weight, 'in_proj_bias': in_proj_bias, 'out_proj_weight': out_proj_weight, 'out_proj_bias': out_proj_bias}
    _L0_attn_all = _L0_attn_setup()
    _L0_attn_in = {k: v for k, v in _L0_attn_all.items() if k in ('in_proj_weight', 'in_proj_bias', 'out_proj_weight', 'out_proj_bias')}
    del _L0_attn_all

    def _L0_ffn_setup():
        import jax, jax.numpy as jnp
        import numpy as np
        EMB = 256
        FF = 4 * EMB

        def _ternary(w):
            scale = jnp.maximum(jnp.mean(jnp.abs(w)), 1e-08)
            w_t = jnp.clip(jnp.round(w / scale), -1.0, 1.0)
            return w + jax.lax.stop_gradient(w_t - w)
        key = jax.random.key(seed)
        kx, k1, k2, kb1, kb2 = jax.random.split(key, 5)
        x = jax.random.normal(kx, (4, 512, EMB), dtype=jnp.float32)
        lim1 = 1.0 / np.sqrt(EMB)
        lim2 = 1.0 / np.sqrt(FF)
        W1 = jax.random.uniform(k1, (FF, EMB), jnp.float32, -lim1, lim1)
        b1 = jax.random.uniform(kb1, (FF,), jnp.float32, -lim1, lim1)
        W2 = jax.random.uniform(k2, (EMB, FF), jnp.float32, -lim2, lim2)
        b2 = jax.random.uniform(kb2, (EMB,), jnp.float32, -lim2, lim2)
        return {'x': x, 'W1': W1, 'b1': b1, 'W2': W2, 'b2': b2}
    _L0_ffn_all = _L0_ffn_setup()
    _L0_ffn_in = {k: v for k, v in _L0_ffn_all.items() if k in ('W1', 'b1', 'W2', 'b2')}
    del _L0_ffn_all
    return {'x': x, 'L0_tok_W': _L0_tok_in['W'], 'L0_tok_b': _L0_tok_in['b'], 'L0_attn_in_proj_weight': _L0_attn_in['in_proj_weight'], 'L0_attn_in_proj_bias': _L0_attn_in['in_proj_bias'], 'L0_attn_out_proj_weight': _L0_attn_in['out_proj_weight'], 'L0_attn_out_proj_bias': _L0_attn_in['out_proj_bias'], 'L0_ffn_W1': _L0_ffn_in['W1'], 'L0_ffn_b1': _L0_ffn_in['b1'], 'L0_ffn_W2': _L0_ffn_in['W2'], 'L0_ffn_b2': _L0_ffn_in['b2']}

def reference(x, L0_tok_W, L0_tok_b, L0_attn_in_proj_weight, L0_attn_in_proj_bias, L0_attn_out_proj_weight, L0_attn_out_proj_bias, L0_ffn_W1, L0_ffn_b1, L0_ffn_W2, L0_ffn_b2):
    import jax
    import jax.numpy as jnp

    def _L0_tok_ref(seq, W, b):
        import jax, jax.numpy as jnp
        import numpy as np
        VOCAB = 50257
        HIDDEN = 256
        out = jnp.take(W, seq, axis=1)
        out = jnp.moveaxis(out, 0, -1) + b
        return out

    def _L0_attn_ref(query, in_proj_weight, in_proj_bias, out_proj_weight, out_proj_bias):
        import jax, jax.numpy as jnp
        import numpy as np
        NUM_HEADS = 16
        S, B, E = query.shape
        H = NUM_HEADS
        hd = E // H
        scale = hd ** (-0.5)
        lin = jnp.einsum('sbe,fe->sbf', query, in_proj_weight) + in_proj_bias
        lin = lin.reshape(S, B * H, 3, hd)
        q = lin[:, :, 0, :]
        k = lin[:, :, 1, :]
        v = lin[:, :, 2, :]
        scores = jnp.einsum('sbd,tbd->bst', q, k) * scale
        attn = jax.nn.softmax(scores.astype(jnp.float32), axis=-1).astype(scores.dtype)
        ctx = jnp.einsum('bst,tbd->sbd', attn, v).reshape(S, B, E)
        out = jnp.einsum('sbe,fe->sbf', ctx, out_proj_weight) + out_proj_bias
        return out

    def _L0_ffn_ref(x, W1, b1, W2, b2):
        import jax, jax.numpy as jnp
        import numpy as np
        EMB = 256
        FF = 4 * EMB

        def _ternary(w):
            scale = jnp.maximum(jnp.mean(jnp.abs(w)), 1e-08)
            w_t = jnp.clip(jnp.round(w / scale), -1.0, 1.0)
            return w + jax.lax.stop_gradient(w_t - w)
        h = jnp.einsum('bsd,fd->bsf', x, _ternary(W1)) + b1
        h = jax.nn.gelu(h, approximate=False)
        out = jnp.einsum('bsf,df->bsd', h, _ternary(W2)) + b2
        return out
    h = _L0_tok_ref(x, L0_tok_W, L0_tok_b)
    h = h + _L0_attn_ref(_layernorm(h, axis=-1), L0_attn_in_proj_weight, L0_attn_in_proj_bias, L0_attn_out_proj_weight, L0_attn_out_proj_bias)
    h = h + _L0_ffn_ref(_layernorm(h, axis=-1), L0_ffn_W1, L0_ffn_b1, L0_ffn_W2, L0_ffn_b2)
    return h

_drawn_inputs = setup_inputs


def setup_inputs(seed=0):
    import zlib

    import numpy as np

    out = dict(_drawn_inputs(seed))
    spreads = {'L0_attn_in_proj_bias': (0.0, 0.1), 'L0_attn_out_proj_bias': (0.0, 0.1)}
    factors = {'L0_ffn_b1': 22.512, 'L0_ffn_b2': 64.0}
    for name, (base, spread) in spreads.items():
        noise = np.random.default_rng([zlib.crc32(name.encode()), seed]).standard_normal(out[name].shape)
        drawn = base * np.exp(spread * noise) if base else spread * noise
        out[name] = jnp.asarray(drawn.astype(out[name].dtype))
    for name, factor in factors.items():
        out[name] = (out[name] * factor).astype(out[name].dtype)
    return out
```

```python
import numpy as np
import concourse.bass as bass
from concourse import mybir
from contextlib import ExitStack

F32 = mybir.dt.float32
F16 = mybir.dt.float16
BF16 = mybir.dt.bfloat16
I32 = mybir.dt.int32
ALU = mybir.AluOpType
ACT = mybir.ActivationFunctionType
X = mybir.AxisListType.X

P = 128
S, B, E = 16, 256, 256
NH, HD = 16, 16
FF = 4 * E
VOCAB = 50257
KT = E // P
T = 2
CT = T * P
TOK = S * B
NC = TOK // CT
G = P // 32
HG = P // HD
HQ = 4
SW = NH * 32
FB = FF // P
BT = 4
NB = TOK // (BT * P)
SCALE = HD ** -0.5
EPS = 1e-5
FAR = -1e30

COL_BQ, COL_BK, COL_BV, COL_B1, COL_HEAD = 0, 2, 4, 6, 14
N_COLS = COL_HEAD + HG
ROW_TOK, ROW_BO, ROW_B2 = 0, 1, 2


def build(nc, idx, table, rows, cols, wq, wk, wv, wo, w1, w2, ident, mask_l, mask_r, out):
    with ExitStack() as ctx:
        def sb(name, shape, dt=F32):
            return ctx.enter_context(nc.sbuf_tensor(name, shape, dt))

        def pb(name, shape):
            return ctx.enter_context(nc.psum_tensor(name, shape, F32))

        def sem(name):
            return ctx.enter_context(nc.semaphore(name))

        idx_sb = sb("idx_sb", [P, NC * T], I32)
        hid = sb("hid", [P, NC * CT * E // P])
        bias_rows = sb("bias_rows", [P, 3, T * E])
        cols_sb = sb("cols_sb", [P, N_COLS])
        wq_sb = sb("wq_sb", [P, KT, E])
        wk_sb = sb("wk_sb", [P, KT, E])
        wv_sb = sb("wv_sb", [P, KT, E])
        wo_sb = sb("wo_sb", [P, KT, E])
        w1_sb = sb("w1_sb", [P, KT * FF])
        w2_sb = sb("w2_sb", [P, FB * E])
        t1 = sb("t1", [P, KT * FF], BF16)
        t2 = sb("t2", [P, FB * E], BF16)
        id_sb = sb("id_sb", [P, P])
        ml_sb = sb("ml_sb", [2, P])
        mr_sb = sb("mr_sb", [2, SW])
        ml_bf = sb("ml_bf", [2, P], BF16)
        mr_bf = sb("mr_bf", [2, SW], BF16)
        ones = sb("ones", [P, P])
        expo = sb("expo", [P, T])
        part_sum = sb("part_sum", [P, 2, 16])
        abs_sum = sb("abs_sum", [P, 2])
        limit = sb("limit", [P, 2])
        neg_limit = sb("neg_limit", [P, 2])
        above = sb("above", [P, 2, P])
        below = sb("below", [P, 2, P])
        stats1 = sb("stats1", [P, T, 6])
        stats2 = sb("stats2", [P, T, 6])
        mom1 = sb("mom1", [P, T, 2])
        mom2 = sb("mom2", [P, T, 2])
        var1 = sb("var1", [P, T])
        var2 = sb("var2", [P, T])
        rstd1 = sb("rstd1", [P, T])
        rstd2 = sb("rstd2", [P, T])
        n1 = sb("n1", [P, T, E])
        n2 = sb("n2", [P, T, E])
        n1_t = sb("n1_t", [P, KT, CT])
        q_t = sb("q_t", [P, KT, CT])
        k_t = sb("k_t", [P, KT, CT])
        k_x = sb("k_x", [P, KT, HG, CT])
        v_x = sb("v_x", [P, T, G, HQ, NH // HQ * HD])
        row_max = sb("row_max", [P, T, NH])
        shifted = sb("shifted", [P, T, SW])
        prob = sb("prob", [P, T, SW])
        row_sum = sb("row_sum", [P, T * NH])
        row_inv = sb("row_inv", [P, T * NH])
        prob_t = sb("prob_t", [P, T, SW])
        ctx_n = sb("ctx_n", [P, T, E])
        ctx_t = sb("ctx_t", [P, KT, CT])
        n2_hi = sb("n2_hi", [P, KT, TOK], F16)
        n2_lo = sb("n2_lo", [P, KT, TOK], F16)
        act = sb("act", [P, 2, BT * P])
        act_hi = sb("act_hi", [P, 2, FB, BT * P], F16)
        act_lo = sb("act_lo", [P, 2, FB, BT * P], F16)
        y = sb("y", [P, 2, BT, E])

        ps = [pb(f"ps{i}", [P, 512]) for i in range(8)]
        ps_scores = ps[0:2]
        ps_nv = ps[2]
        ps_q = ps[3]
        ps_k = ps[4]
        ps_pt = [ps_q, ps_k]
        ps_ctx = ps[5]
        ps_ct = ps[6]
        ps_on = ps[7]

        idx_landed, rows_landed_dma, cols_landed = sem("idx_landed"), sem("rows_dma"), sem("cols_landed")
        wqk_landed, wvo_landed, wff_landed, const_landed = (sem(n) for n in ("wqk", "wvo", "wff", "const"))
        gathered = [sem(f"gathered{c}") for c in range(NC)]
        names = """emb_landed h_biased stats1_done moments1 var1_ready rstd1_ready n1_ready hbo_ready
            nt_done nts_ready q_done qs_ready k_done ks_ready kx_ready v_done vx_ready
            scores_done max_done shift_done exp_done sum_done inv_done pt_done pts_ready ctx_done ctxn_ready
            ct_done cts_ready attn_done h1_ready stats2_done moments2 var2_ready rstd2_ready n2_ready hb2_ready
            n2t_done n2hi_ready n2lo_ready
            zeroed masks_ready abs_part abs_ready abs_total limit_ready neg_limit_ready cmp_done tern_ready
            up_done gelu_done hi_done lo_done down_done y_ready y_stored0 y_stored1"""
        s = {n: sem(n) for n in names.split()}

        (emb_landed, h_biased, stats1_done, moments1, var1_ready, rstd1_ready, n1_ready, hbo_ready,
         nt_done, nts_ready, q_done, qs_ready, k_done, ks_ready, kx_ready, v_done, vx_ready,
         scores_done, max_done, shift_done, exp_done, sum_done, inv_done, pt_done, pts_ready, ctx_done,
         ctxn_ready, ct_done, cts_ready, attn_done, h1_ready, stats2_done, moments2, var2_ready,
         rstd2_ready, n2_ready, hb2_ready, n2t_done, n2hi_ready, n2lo_ready,
         zeroed, masks_ready, abs_part, abs_ready, abs_total, limit_ready, neg_limit_ready, cmp_done,
         tern_ready, up_done, gelu_done, hi_done, lo_done, down_done, y_ready, y_stored0,
         y_stored1) = s.values()
        y_stored = [y_stored0, y_stored1]
        closed_off, expo_ready = sem("closed_off"), sem("expo_ready")

        LEAD, LAG = 2, 2

        def live(j):
            return not isinstance(j, int) or 0 <= j < NC

        def upto(j, per=1):
            return per * j + per

        def lone(eng):
            eng.wait_ge(idx_landed, 16).then_inc(closed_off, 1)

        def tile(j, t):
            return bass.ds((j * T + t) * E, E)

        def chunk(j):
            return bass.ds(j * (T * E), T * E)

        def steps(eng, step):
            for c in range(-LEAD, LAG):
                step(c)
            with eng.Fori(LAG, NC - LEAD) as c:
                step(c)
            for c in range(NC - LEAD, NC + LAG):
                step(c)

        block = ctx.enter_context(nc.Block())

        @block.sync
        def _(sp):
            sp.dma_start(idx_sb[:], idx).then_inc(idx_landed, 16)
            sp.dma_start(bias_rows[:], rows).then_inc(rows_landed_dma, 16)
            sp.dma_start(wq_sb[:], wq).then_inc(wqk_landed, 16)
            sp.dma_start(wk_sb[:], wk).then_inc(wqk_landed, 16)
            sp.dma_start(wv_sb[:], wv).then_inc(wvo_landed, 16)
            sp.dma_start(wo_sb[:], wo).then_inc(wvo_landed, 16)
            sp.dma_start(w1_sb[:], w1).then_inc(wff_landed, 16)
            sp.dma_start(w2_sb[:], w2).then_inc(wff_landed, 16)
            for c in range(NC):
                sp.wait_ge(gathered[c], 16 * T).then_inc(emb_landed, 1)
            out_v = out.rearrange("(m t p) e -> m p t e", t=BT, p=P)

            def store(i, b, m):
                sp.wait_ge(y_ready, upto(m))
                lone(sp)
                sp.dma_start(out_v[bass.ds(m, 1)].rearrange("o p t e -> p (o t) e"), y[:, b]).then_inc(y_stored[b], 16)

            with sp.Fori(0, NB // 2) as i:
                for b in range(2):
                    store(i, b, 2 * i + b)
            for b in range(2):
                sp.wait_ge(y_stored[b], 16 * (NB // 2))

        @block.gpsimd
        def _(pool):
            pool.wait_ge(idx_landed, 16)

            def gather(c):
                for t in range(T * c, T * c + T):
                    nc.gpsimd.indirect_dma_start(
                        hid[:, t * E:(t + 1) * E], None, table,
                        bass.IndirectOffsetOnAxis(ap=idx_sb[:, t:t + 1], axis=0),
                    ).then_inc(gathered[c], 16)

            def add_row(j, row):
                return nc.gpsimd.tensor_tensor(hid[:, chunk(j)], hid[:, chunk(j)], bias_rows[:, row, :], ALU.add)

            def inverse_deviation(mom, var, rstd, var_ready, rstd_ready, j):
                nc.gpsimd.tensor_scalar(var[:], mom[:, :, 1], EPS, None, ALU.add).then_inc(var_ready, 1)
                pool.wait_ge(var_ready, upto(j))
                lone(pool)
                nc.gpsimd.tensor_tensor(rstd[:], var[:], expo[:], ALU.pow).then_inc(rstd_ready, 1)

            def step(c):
                if live(c + 3):
                    pool.wait_ge(emb_landed, upto(c + 3))
                    lone(pool)
                    add_row(c + 3, ROW_TOK).then_inc(h_biased, 1)
                if live(c + 2):
                    pool.wait_ge(moments1, upto(c + 2))
                    if live(c + 1):
                        pool.wait_ge(n1_ready, upto(c + 1))
                    lone(pool)
                    inverse_deviation(mom1, var1, rstd1, var1_ready, rstd1_ready, c + 2)
                if live(c - 1):
                    pool.wait_ge(moments2, upto(c - 1))
                    if live(c - 2):
                        pool.wait_ge(n2_ready, upto(c - 2))
                    lone(pool)
                    inverse_deviation(mom2, var2, rstd2, var2_ready, rstd2_ready, c - 1)
                if live(c + 2):
                    pool.wait_ge(n1_ready, upto(c + 2))
                    lone(pool)
                    add_row(c + 2, ROW_BO).then_inc(hbo_ready, 1)
                if live(c - 1):
                    pool.wait_ge(n2_ready, upto(c - 1))
                    lone(pool)
                    add_row(c - 1, ROW_B2).then_inc(hb2_ready, 1)
                if live(c):
                    pool.wait_ge(cmp_done, upto(c))
                    lone(pool)
                    for w, dst in enumerate((t1, t2)):
                        last = nc.gpsimd.tensor_tensor(dst[:, bass.ds(c * P, P)], above[:, w, :], below[:, w, :],
                                                       ALU.subtract)
                    last.then_inc(tern_ready, 1)

            for c in range(3):
                gather(c)
            nc.gpsimd.memset(expo[:], -0.5).then_inc(expo_ready, 1)
            pool.wait_ge(expo_ready, 1)
            pool.wait_ge(rows_landed_dma, 16)
            pool.wait_ge(emb_landed, 1)
            add_row(0, ROW_TOK).then_inc(h_biased, 1)
            for c in range(-LEAD, 0):
                step(c)
            for c in range(3, 9):
                gather(c)
            step(0)
            for c in range(9, NC):
                gather(c)
            step(1)
            with pool.Fori(LAG, NC - 3) as c:
                step(c)
            for c in range(NC - 3, NC + LAG):
                step(c)

        @block.vector
        def _(dve):
            def moments(stats, mom, done):
                for t in range(T):
                    last = nc.vector.bn_aggr(mom[:, t, :], stats[:, t, :])
                last.then_inc(done, 1)

            def normalise(n, mom, rstd, j, ready):
                for t in range(T):
                    last = nc.vector.tensor_scalar(n[:, t, :], hid[:, tile(j, t)], mom[:, t, 0:1],
                                                   rstd[:, t:t + 1], ALU.subtract, ALU.mult)
                last.then_inc(ready, 1)

            def step(c):
                if live(c - 2):
                    dve.wait_ge(n2hi_ready, upto(c - 2))
                    at = bass.ds((c - 2) * CT, CT)
                    nc.vector.tensor_tensor(n2_lo[:, :, at], ps_on[:].rearrange("p (k n) -> p k n", k=KT),
                                            n2_hi[:, :, at], ALU.subtract).then_inc(n2lo_ready, 1)
                if live(c):
                    if live(c - 1):
                        dve.wait_ge(shift_done, upto(c - 1, T))
                    for t in range(T):
                        dve.wait_ge(scores_done, c * T + t + 1)
                        nc.vector.tensor_reduce(row_max[:, t, :], ps_scores[t][:].rearrange("p (h k) -> p h k", k=32),
                                                X, ALU.max).then_inc(max_done, 1)
                    for t in range(T):
                        if live(c - 1):
                            dve.wait_ge(exp_done, (c - 1) * T + t + 1)
                        dve.wait_ge(max_done, c * T + t + 1)
                        nc.vector.tensor_tensor(shifted[:, t, :].rearrange("p (h k) -> p h k", k=32),
                                                ps_scores[t][:].rearrange("p (h k) -> p h k", k=32),
                                                row_max[:, t, :].unsqueeze(2).to_broadcast([P, NH, 32]),
                                                ALU.subtract).then_inc(shift_done, 1)
                if live(c + 2):
                    dve.wait_ge(h_biased, upto(c + 2))
                    if live(c + 1):
                        dve.wait_ge(moments1, upto(c + 1))
                    lone(dve)
                    for t in range(T):
                        last = nc.vector.bn_stats(stats1[:, t, :], hid[:, tile(c + 2, t)])
                    last.then_inc(stats1_done, 1)
                if live(c + 2):
                    dve.wait_ge(stats1_done, upto(c + 2))
                    if live(c + 1):
                        dve.wait_ge(n1_ready, upto(c + 1))
                        dve.wait_ge(rstd1_ready, upto(c + 1))
                    lone(dve)
                    moments(stats1, mom1, moments1)
                if live(c - 1):
                    dve.wait_ge(hbo_ready, upto(c - 1))
                    dve.wait_ge(attn_done, upto(c - 1))
                    nc.vector.tensor_tensor(hid[:, chunk(c - 1)], ps_on[:], hid[:, chunk(c - 1)], ALU.add)\
                        .then_inc(h1_ready, 1)
                if live(c + 1):
                    dve.wait_ge(ks_ready, upto(c + 1))
                    if live(c):
                        dve.wait_ge(scores_done, upto(c, T))
                    for j in range(HG):
                        last = nc.vector.tensor_scalar(k_x[:, :, j, :], k_t[:],
                                                       cols_sb[:, COL_HEAD + j:COL_HEAD + j + 1], None, ALU.mult)
                    last.then_inc(kx_ready, 1)
                if live(c - 1):
                    dve.wait_ge(h1_ready, upto(c - 1))
                    if live(c - 2):
                        dve.wait_ge(moments2, upto(c - 2))
                    lone(dve)
                    for t in range(T):
                        last = nc.vector.bn_stats(stats2[:, t, :], hid[:, tile(c - 1, t)])
                    last.then_inc(stats2_done, 1)
                if live(c):
                    dve.wait_ge(exp_done, upto(c, T))
                    if live(c - 1):
                        dve.wait_ge(inv_done, upto(c - 1))
                    nc.vector.tensor_reduce(row_sum[:], prob[:].rearrange("p t (h k) -> p (t h) k", k=32), X, ALU.add)\
                        .then_inc(sum_done, 1)
                if live(c - 1):
                    dve.wait_ge(stats2_done, upto(c - 1))
                    if live(c - 2):
                        dve.wait_ge(n2_ready, upto(c - 2))
                        dve.wait_ge(rstd2_ready, upto(c - 2))
                    lone(dve)
                    moments(stats2, mom2, moments2)
                if live(c):
                    dve.wait_ge(sum_done, upto(c))
                    if live(c - 1):
                        dve.wait_ge(ctxn_ready, upto(c - 1))
                    nc.vector.reciprocal(row_inv[:], row_sum[:]).then_inc(inv_done, 1)
                if live(c):
                    if not isinstance(c, int) or c >= 1:
                        dve.wait_ge(tern_ready, upto(c - 1))
                    for w, src in enumerate((w1_sb, w2_sb)):
                        part = src[:, bass.ds(c * P, P)]
                        nc.vector.tensor_scalar(above[:, w, :], part, limit[:, w:w + 1], None, ALU.is_gt)
                        last = nc.vector.tensor_scalar(below[:, w, :], part, neg_limit[:, w:w + 1], None, ALU.is_lt)
                    last.then_inc(cmp_done, 1)
                if live(c + 2):
                    dve.wait_ge(rstd1_ready, upto(c + 2))
                    if live(c + 1):
                        dve.wait_ge(nt_done, upto(c + 1))
                    normalise(n1, mom1, rstd1, c + 2, n1_ready)
                if live(c - 1):
                    dve.wait_ge(rstd2_ready, upto(c - 1))
                    if live(c - 2):
                        dve.wait_ge(n2t_done, upto(c - 2))
                    normalise(n2, mom2, rstd2, c - 1, n2_ready)
                if live(c):
                    dve.wait_ge(inv_done, upto(c))
                    dve.wait_ge(ctx_done, upto(c))
                    if live(c - 1):
                        dve.wait_ge(ct_done, upto(c - 1))
                    nc.vector.tensor_tensor(ctx_n[:].rearrange("p t (h d) -> p (t h) d", d=HD),
                                            ps_ctx[:].rearrange("p (h d) -> p h d", d=HD),
                                            row_inv[:].unsqueeze(2).to_broadcast([P, T * NH, HD]),
                                            ALU.mult).then_inc(ctxn_ready, 1)

            nc.vector.memset(v_x[:], 0.0)
            nc.vector.memset(ones[:], 1.0).then_inc(zeroed, 1)
            dve.wait_ge(const_landed, 48)
            nc.vector.tensor_copy(ml_bf[:], ml_sb[:])
            nc.vector.tensor_copy(mr_bf[:], mr_sb[:]).then_inc(masks_ready, 1)
            dve.wait_ge(cols_landed, 16)
            dve.wait_ge(idx_landed, 16)
            step(-2)
            step(-1)
            dve.wait_ge(wff_landed, 32)
            for w, src in enumerate((w1_sb, w2_sb)):
                nc.vector.tensor_reduce(part_sum[:, w, :], src[:].rearrange("p (a n) -> p a n", a=16), X, ALU.add,
                                        apply_absolute_value=True).then_inc(abs_part, 1)
            dve.wait_ge(abs_part, 2)
            nc.vector.tensor_reduce(abs_sum[:], part_sum[:], X, ALU.add).then_inc(abs_ready, 1)
            dve.wait_ge(abs_total, 1)
            nc.vector.tensor_scalar(limit[:], ps_ctx[:, 0:2], 1.0 / (FF * E), 1e-8, ALU.mult, ALU.max)\
                .then_inc(limit_ready, 1)
            dve.wait_ge(limit_ready, 1)
            nc.vector.tensor_scalar(neg_limit[:], limit[:], -0.5, None, ALU.mult).then_inc(limit_ready, 1)
            dve.wait_ge(limit_ready, 2)
            nc.vector.tensor_scalar(limit[:], limit[:], 0.5, None, ALU.mult).then_inc(neg_limit_ready, 1)
            dve.wait_ge(neg_limit_ready, 1)
            step(0)
            step(1)
            with dve.Fori(LAG, NC - LEAD) as c:
                step(c)
            for c in range(NC - LEAD, NC + LAG):
                step(c)

            def parts(b, m, f):
                slot = f % 2
                n = m * FB + f + 1
                dve.wait_ge(gelu_done, n)
                if not isinstance(m, int) or m >= 2:
                    dve.wait_ge(down_done, (m - 1) * BT)
                nc.vector.tensor_copy(act_hi[:, b, f, :], act[:, slot, :]).then_inc(hi_done, 1)
                dve.wait_ge(hi_done, n)
                nc.vector.tensor_tensor(act_lo[:, b, f, :], act[:, slot, :], act_hi[:, b, f, :], ALU.subtract)\
                    .then_inc(lo_done, 1)

            def finish(b, m, t):
                dve.wait_ge(down_done, m * BT + t + 1)
                if (not isinstance(m, int) or m >= 2) and t == 0:
                    dve.wait_ge(y_stored[b], 8 * (m - b))
                last = nc.vector.tensor_tensor(y[:, b, t, :], ps[4 + t][:, 0:E],
                                               hid[:, bass.ds((m * BT + t) * E, E)], ALU.add)
                if t == BT - 1:
                    last.then_inc(y_ready, 1)

            dve.wait_ge(hb2_ready, NC)

            def block_step(b, m):
                for f in range(FB):
                    parts(b, m, f)
                    if f % 2 == 1 and (not isinstance(m, int) or m >= 1):
                        finish(1 - b, m - 1, f // 2)

            for b in range(2):
                block_step(b, b)
            with dve.Fori(1, NB // 2) as i:
                for b in range(2):
                    block_step(b, 2 * i + b)
            for t in range(BT):
                finish(1, NB - 1, t)

        @block.scalar
        def _(act_e):
            act_e.dma_start(id_sb[:], ident).then_inc(const_landed, 16)
            act_e.dma_start(ml_sb[:], mask_l).then_inc(const_landed, 16)
            act_e.dma_start(mr_sb[:], mask_r).then_inc(const_landed, 16)
            act_e.dma_start(cols_sb[:], cols).then_inc(cols_landed, 16)
            act_e.wait_ge(idx_landed, 16)
            act_e.wait_ge(cols_landed, 16)

            def with_bias(dst, src, col, ready):
                for g in range(KT):
                    last = nc.scalar.activation(dst[:, g, :], src[:, g * CT:(g + 1) * CT], ACT.Identity,
                                                bias=cols_sb[:, col + g:col + g + 1])
                last.then_inc(ready, 1)

            def exps(c, t):
                act_e.wait_ge(shift_done, c * T + t + 1)
                if live(c - 1):
                    act_e.wait_ge(sum_done, upto(c - 1))
                    act_e.wait_ge(pt_done, (c - 1) * T + t + 1)
                nc.scalar.activation(prob[:, t, :], shifted[:, t, :], ACT.Exp, scale=SCALE).then_inc(exp_done, 1)

            def step(c):
                if live(c - 2):
                    act_e.wait_ge(n2t_done, upto(c - 2))
                    lone(act_e)
                    nc.scalar.activation(n2_hi[:, :, bass.ds((c - 2) * CT, CT)],
                                         ps_on[:].rearrange("p (k n) -> p k n", k=KT), ACT.Copy)\
                        .then_inc(n2hi_ready, 1)
                if live(c):
                    exps(c, 0)
                if live(c + 1):
                    act_e.wait_ge(nt_done, upto(c + 1))
                    if live(c):
                        act_e.wait_ge(v_done, upto(c))
                    nc.scalar.activation(n1_t[:].rearrange("p k n -> p (k n)"), ps_nv[:], ACT.Copy)\
                        .then_inc(nts_ready, 1)
                if live(c):
                    exps(c, 1)
                if live(c + 1):
                    act_e.wait_ge(q_done, upto(c + 1))
                    with_bias(q_t, ps_q, COL_BQ, qs_ready)
                    act_e.wait_ge(k_done, upto(c + 1))
                    if live(c):
                        act_e.wait_ge(kx_ready, upto(c))
                    with_bias(k_t, ps_k, COL_BK, ks_ready)
                if live(c):
                    for t in range(T):
                        act_e.wait_ge(pt_done, c * T + t + 1)
                        if live(c - 1):
                            act_e.wait_ge(ctx_done, upto(c - 1))
                        nc.scalar.activation(prob_t[:, t, :], ps_pt[t][:], ACT.Copy).then_inc(pts_ready, 1)
                    act_e.wait_ge(ct_done, upto(c))
                    if live(c - 1):
                        act_e.wait_ge(attn_done, upto(c - 1))
                    with_bias(ctx_t, ps_ct, COL_BV, cts_ready)
                if live(c + 1):
                    act_e.wait_ge(v_done, upto(c + 1))
                    if live(c):
                        act_e.wait_ge(ctx_done, upto(c))
                    for g in range(G):
                        for a in range(HQ):
                            src = ps_nv[32 * g:32 * g + 32, :].rearrange("p (t a n) -> p t a n", t=T, a=HQ)
                            last = nc.scalar.activation(v_x[32 * a:32 * a + 32, :, g, a, :], src[:, :, a, :], ACT.Copy)
                    last.then_inc(vx_ready, 1)

            act_e.wait_ge(zeroed, 1)
            steps(act_e, step)

            def block_step(b, m):
                for f in range(FB):
                    slot = f % 2
                    n = m * FB + f + 1
                    act_e.wait_ge(up_done, n)
                    if (not isinstance(m, int) or m >= 1) or f >= 2:
                        act_e.wait_ge(lo_done, n - 2)
                    nc.scalar.activation(act[:, slot, :], ps[f % 4][:], ACT.Gelu,
                                         bias=cols_sb[:, COL_B1 + f:COL_B1 + f + 1]).then_inc(gelu_done, 1)

            for b in range(2):
                block_step(b, b)
            with act_e.Fori(1, NB // 2) as i:
                for b in range(2):
                    block_step(b, 2 * i + b)

        @block.tensor
        def _(pe):
            def mm(o, l, r, start, stop, **kw):
                return nc.tensor.matmul(o, l, r, start=start, stop=stop, **kw)

            def scores(c, t):
                pe.wait_ge(kx_ready, upto(c))
                pe.wait_ge(qs_ready, upto(c))
                if live(c - 1):
                    pe.wait_ge(shift_done, (c - 1) * T + t + 1)
                mm(ps_scores[t][:], ml_bf[:], mr_bf[:], True, False)
                for k in range(KT):
                    for g in range(G):
                        at = slice(t * P + 32 * g, t * P + 32 * g + 32)
                        last = mm(ps_scores[t][32 * g:32 * g + 32, k * 256:(k + 1) * 256]
                                  .rearrange("p (h n) -> p h n", h=HG),
                                  q_t[:, k, at], k_x[:, k, :, at], False, k == KT - 1)
                last.then_inc(scores_done, 1)

            def attn_out(j):
                pe.wait_ge(cts_ready, upto(j))
                if live(j - 1):
                    pe.wait_ge(n2lo_ready, upto(j - 1))
                for t in range(T):
                    for k in range(KT):
                        last = mm(ps_on[:, t * E:(t + 1) * E], ctx_t[:, k, t * P:(t + 1) * P], wo_sb[:, k, :],
                                  k == 0, k == KT - 1)
                last.then_inc(attn_done, 1)

            def transposes(dst, src):
                for k in range(KT):
                    for t in range(T):
                        last = nc.tensor.transpose(dst[:, k * CT + t * P:k * CT + (t + 1) * P],
                                                   src[:, t, k * P:(k + 1) * P], id_sb[:])
                return last

            def project(dst, w):
                for g in range(KT):
                    for k in range(KT):
                        last = mm(dst[:, g * CT:(g + 1) * CT], w[:, k, g * P:(g + 1) * P], n1_t[:, k, :],
                                  k == 0, k == KT - 1)
                return last

            def step(c):
                if live(c):
                    for t in range(T):
                        scores(c, t)
                if live(c - 1):
                    attn_out(c - 1)
                if live(c + 1):
                    pe.wait_ge(n1_ready, upto(c + 1))
                    if live(c):
                        pe.wait_ge(vx_ready, upto(c))
                    transposes(ps_nv, n1).then_inc(nt_done, 1)
                    pe.wait_ge(nts_ready, upto(c + 1))
                    if live(c - 1):
                        pe.wait_ge(pts_ready, upto(c - 1, T))
                    project(ps_q, wq_sb).then_inc(q_done, 1)
                    project(ps_k, wk_sb).then_inc(k_done, 1)
                if live(c):
                    for t in range(T):
                        pe.wait_ge(exp_done, c * T + t + 1)
                        if live(c + 1):
                            pe.wait_ge([qs_ready, ks_ready][t], upto(c + 1))
                        for a in range(SW // P):
                            last = nc.tensor.transpose(ps_pt[t][:, a * P:(a + 1) * P],
                                                       prob[:, t, a * P:(a + 1) * P], id_sb[:])
                        last.then_inc(pt_done, 1)
                    if live(c - 1):
                        pe.wait_ge(ctxn_ready, upto(c - 1))
                    pe.wait_ge(vx_ready, upto(c))
                    for t in range(T):
                        pe.wait_ge(pts_ready, c * T + t + 1)
                        for a in range(SW // P):
                            for g in range(G):
                                last = mm(ps_ctx[32 * g:32 * g + 32, t * E + a * 64:t * E + (a + 1) * 64]
                                          .rearrange("p (h d) -> p h d", h=HQ),
                                          prob_t[:, t, a * P + 32 * g:a * P + 32 * g + 32],
                                          v_x[:, t, g, :, a * HD:(a + 1) * HD], True, True)
                    last.then_inc(ctx_done, 1)
                if live(c + 1):
                    pe.wait_ge(nts_ready, upto(c + 1))
                    for t in range(T):
                        for k in range(KT):
                            last = mm(ps_nv[:, t * E:(t + 1) * E], n1_t[:, k, t * P:(t + 1) * P], wv_sb[:, k, :],
                                      k == 0, k == KT - 1)
                    last.then_inc(v_done, 1)
                if live(c):
                    pe.wait_ge(ctxn_ready, upto(c))
                    if live(c - 1):
                        pe.wait_ge(cts_ready, upto(c - 1))
                    transposes(ps_ct, ctx_n).then_inc(ct_done, 1)
                if live(c - 1):
                    pe.wait_ge(n2_ready, upto(c - 1))
                    transposes(ps_on, n2).then_inc(n2t_done, 1)

            pe.wait_ge(const_landed, 48)
            pe.wait_ge(masks_ready, 1)
            pe.wait_ge(zeroed, 1)
            step(-2)
            pe.wait_ge(wqk_landed, 32)
            pe.wait_ge(wvo_landed, 32)
            step(-1)
            pe.wait_ge(abs_ready, 1)
            mm(ps_ctx[:, 0:2], ones[:], abs_sum[:], True, True).then_inc(abs_total, 1)
            pe.wait_ge(limit_ready, 1)
            step(0)
            step(1)
            with pe.Fori(LAG, NC - LEAD) as c:
                step(c)
            for c in range(NC - LEAD, NC + LAG):
                step(c)

            pe.wait_ge(tern_ready, NC)
            pe.wait_ge(n2lo_ready, upto(NC - 1))
            pe.wait_ge(shift_done, upto(NC - 1, T))

            def up(m, f):
                n = m * FB + f + 1
                if (not isinstance(m, int) or m >= 1) or f >= 4:
                    pe.wait_ge(gelu_done, n - 4)
                at = bass.ds(m * BT * P, BT * P)
                for i, part in enumerate((n2_hi, n2_lo)):
                    for k in range(KT):
                        last = mm(ps[f % 4][:], t1[:, k * FF + f * P:k * FF + (f + 1) * P], part[:, k, at],
                                  i + k == 0, i + k == 2)
                last.then_inc(up_done, 1)

            def down(b, m, f, t, half):
                if half == 0:
                    if t == 0:
                        pe.wait_ge(lo_done, m * FB + FB)
                    if not isinstance(m, int) or m >= 1:
                        pe.wait_ge(y_ready, upto(m - 1))
                for f in range(half * FB // 2, (half + 1) * FB // 2):
                    for i, part in enumerate((act_hi, act_lo)):
                        last = mm(ps[4 + t][:, 0:E], part[:, b, f, t * P:(t + 1) * P], t2[:, f * E:(f + 1) * E],
                                  f + i == 0, f == FB - 1 and i == 1)
                if half == 1:
                    last.then_inc(down_done, 1)

            def block_step(b, m):
                for f in range(FB):
                    up(m, f)
                    if not isinstance(m, int) or m >= 1:
                        down(1 - b, m - 1, f, f // 2, f % 2)

            for b in range(2):
                block_step(b, b)
            with pe.Fori(1, NB // 2) as i:
                for b in range(2):
                    block_step(b, 2 * i + b)
            for f in range(FB):
                down(1, NB - 1, f, f // 2, f % 2)


def kernel(x, L0_tok_W, L0_tok_b, L0_attn_in_proj_weight, L0_attn_in_proj_bias, L0_attn_out_proj_weight,
           L0_attn_out_proj_bias, L0_ffn_W1, L0_ffn_b1, L0_ffn_W2, L0_ffn_b2):
    import concourse.bacc as bacc
    from concourse.bass_utils import run_bass_kernel_spmd

    arr = np.asarray
    cont = np.ascontiguousarray

    def contract(w):
        w = arr(w)
        return cont(w.reshape(w.shape[0] // P, P, w.shape[1]).transpose(1, 0, 2))

    def by_partition(v):
        return cont(arr(v).reshape(-1, P).T)

    idx = cont(arr(x).T.reshape(NC * T, P).T)
    w_in = arr(L0_attn_in_proj_weight).reshape(NH, 3, HD, E)
    b_in = arr(L0_attn_in_proj_bias).reshape(NH, 3, HD)
    w_v = w_in[:, 2].reshape(NH // HQ, HQ, HD, E).transpose(1, 0, 2, 3).reshape(E, E)
    head = (np.arange(P)[:, None] // HD == np.arange(HG)[None, :]).astype(np.float32)
    cols = cont(np.concatenate([by_partition(b_in[:, 0]), by_partition(b_in[:, 1]), by_partition(b_in[:, 2]),
                                by_partition(L0_ffn_b1), head], axis=1))
    rows = cont(np.broadcast_to(np.stack([np.concatenate([arr(b), arr(b)]) for b in
                                          (L0_tok_b, L0_attn_out_proj_bias, L0_ffn_b2)]), (P, 3, T * E)))
    entry = np.arange(P) // S % 2
    mask_l = cont((entry[None, :] == np.arange(2)[:, None]).astype(np.float32))
    mask_r = cont(np.where(np.arange(SW)[None, :] // S % 2 == np.arange(2)[:, None], 0.0, FAR).astype(np.float32))
    arrays = {
        "idx": idx,
        "table": cont(arr(L0_tok_W).T),
        "rows": rows,
        "cols": cols,
        "wq": contract(w_in[:, 0].reshape(E, E).T),
        "wk": contract(w_in[:, 1].reshape(E, E).T),
        "wv": contract(w_v.T),
        "wo": contract(arr(L0_attn_out_proj_weight).T),
        "w1": contract(arr(L0_ffn_W1).T).reshape(P, KT * FF),
        "w2": contract(arr(L0_ffn_W2).T).reshape(P, FB * E),
        "ident": np.eye(P, dtype=np.float32),
        "mask_l": mask_l,
        "mask_r": mask_r,
    }
    nc = bacc.Bacc("TRN2", target_bir_lowering=False, num_devices=1)
    aps = [nc.dram_tensor(f"in_{n}", a.shape, mybir.dt.from_np(a.dtype), kind="ExternalInput").ap()
           for n, a in arrays.items()]
    out = nc.dram_tensor("out", (TOK, E), F32, kind="ExternalOutput").ap()
    build(nc, *aps, out)
    r = run_bass_kernel_spmd(nc, [{f"in_{n}": a for n, a in arrays.items()}], core_ids=[0])
    return cont(r.results[0]["out"].reshape(B, S, E).transpose(1, 0, 2))
```

```python
import numpy as np
import concourse.bass as bass
from concourse import mybir
from contextlib import ExitStack

F32 = mybir.dt.float32
F16 = mybir.dt.float16
BF16 = mybir.dt.bfloat16
I32 = mybir.dt.int32
ALU = mybir.AluOpType
ACT = mybir.ActivationFunctionType
X = mybir.AxisListType.X

P = 128
S, B, E = 16, 256, 256
NH, HD = 16, 16
FF = 4 * E
VOCAB = 50257
KT = E // P
T = 2
CT = T * P
TOK = S * B
NC = TOK // CT
G = P // 32
HG = P // HD
HQ = 4
SW = NH * 32
FB = FF // P
BT = 4
NB = TOK // (BT * P)
SCALE = HD ** -0.5
EPS = 1e-5
KX_ACT = 4
FAR = -1e30

COL_BQ, COL_BK, COL_BV, COL_B1, COL_HEAD = 0, 2, 4, 6, 14
N_COLS = COL_HEAD + HG
ROW_TOK, ROW_BO, ROW_B2 = 0, 1, 2


def build(nc, idx, table, rows, cols, wq, wk, wv, wo, w1, w2, ident, mask_l, mask_r, out):
    with ExitStack() as ctx:
        def sb(name, shape, dt=F32):
            return ctx.enter_context(nc.sbuf_tensor(name, shape, dt))

        def sem(name):
            return ctx.enter_context(nc.semaphore(name))

        idx_sb = sb("idx_sb", [P, NC * T], I32)
        hid = sb("hid", [P, NC * CT * E // P])
        bias_rows = sb("bias_rows", [P, 3, T * E])
        cols_sb = sb("cols_sb", [P, N_COLS])
        wq_sb = sb("wq_sb", [P, KT, E])
        wk_sb = sb("wk_sb", [P, KT, E])
        wv_sb = sb("wv_sb", [P, KT, E])
        wo_sb = sb("wo_sb", [P, KT, E])
        w1_sb = sb("w1_sb", [P, KT * FF])
        w2_sb = sb("w2_sb", [P, FB * E])
        t1 = sb("t1", [P, KT * FF], BF16)
        t2 = sb("t2", [P, FB * E], BF16)
        id_sb = sb("id_sb", [P, P])
        ml_sb = sb("ml_sb", [2, P])
        mr_sb = sb("mr_sb", [2, SW])
        ml_bf = sb("ml_bf", [2, P], BF16)
        mr_bf = sb("mr_bf", [2, SW], BF16)
        ones = sb("ones", [P, P])
        warm = sb("warm", [P, 1])
        expo = sb("expo", [P, T])
        part_sum = sb("part_sum", [P, 2, 16])
        abs_sum = sb("abs_sum", [P, 2])
        limit = sb("limit", [P, 2])
        neg_limit = sb("neg_limit", [P, 2])
        above = sb("above", [P, 2, P])
        below = sb("below", [P, 2, P])
        stats1 = sb("stats1", [P, T, 6])
        stats2 = sb("stats2", [P, T, 6])
        mom1 = sb("mom1", [P, T, 2])
        mom2 = sb("mom2", [P, T, 2])
        var1 = sb("var1", [P, T])
        var2 = sb("var2", [P, T])
        rstd1 = sb("rstd1", [P, T])
        rstd2 = sb("rstd2", [P, T])
        n1 = sb("n1", [P, T, E])
        n2 = sb("n2", [P, T, E])
        n1_t = sb("n1_t", [P, KT, CT])
        q_t = sb("q_t", [P, KT, CT])
        k_t = sb("k_t", [P, KT, CT])
        k_x = sb("k_x", [P, KT, HG, CT])
        v_x = sb("v_x", [P, T, G, HQ, NH // HQ * (HD + 1)])
        row_max = sb("row_max", [P, T, NH])
        shifted = sb("shifted", [P, T, SW])
        prob = sb("prob", [P, T, SW])
        row_inv = sb("row_inv", [P, T, NH])
        prob_t = sb("prob_t", [P, T, SW])
        ctx_n = sb("ctx_n", [P, T, E])
        ctx_t = sb("ctx_t", [P, KT, CT])
        n2_hi = sb("n2_hi", [P, KT, TOK], F16)
        n2_lo = sb("n2_lo", [P, KT, TOK], F16)
        act = sb("act", [P, 2, BT * P])
        act_hi = sb("act_hi", [P, 2, FB, BT * P], F16)
        act_lo = sb("act_lo", [P, 2, FB, BT * P], F16)
        y = sb("y", [P, 2, BT, E])

        ps = ctx.enter_context(nc.psum_tensor("ps", [P, 8, 512], F32))
        ps_scores = [ps[:, 0, :], ps[:, 1, :]]
        ps_ctx = ps[:, 0:2, 0:NH * (HD + 1)].rearrange("p t (h d) -> p t h d", d=HD + 1)
        ps_nt = ps[:, 2, :]
        ps_k = ps[:, 3, :]
        ps_q = ps[:, 4, :]
        ps_pt = [ps_k, ps_nt]
        ps_v = ps[:, 5, :]
        ps_ct = ps[:, 6, :]
        ps_on = ps[:, 7, :]

        idx_landed, rows_landed_dma, cols_landed = sem("idx_landed"), sem("rows_dma"), sem("cols_landed")
        wqk_landed, wvo_landed, wff_landed, const_landed = (sem(n) for n in ("wqk", "wvo", "wff", "const"))
        gathered = [sem(f"gathered{c}") for c in range(NC)]
        names = """emb_landed h_biased stats1_done moments1 var1_ready rstd1_ready n1_ready hbo_ready
            nt_done nts_ready q_done qs_ready k_done ks_ready kx_ready v_done vx_ready
            scores_done max_done shift_done exp_done inv_done pt_done pts_ready ctx_done ctxn_ready
            ct_done cts_ready attn_done h1_ready stats2_done moments2 var2_ready rstd2_ready n2_ready hb2_ready
            n2t_done n2hi_ready n2lo_ready
            zeroed masks_ready abs_part abs_ready abs_total limit_ready neg_limit_ready cmp_done tern_ready
            up_done gelu_done hi_done lo_done down_done y_ready y_stored0 y_stored1"""
        s = {n: sem(n) for n in names.split()}

        (emb_landed, h_biased, stats1_done, moments1, var1_ready, rstd1_ready, n1_ready, hbo_ready,
         nt_done, nts_ready, q_done, qs_ready, k_done, ks_ready, kx_ready, v_done, vx_ready,
         scores_done, max_done, shift_done, exp_done, inv_done, pt_done, pts_ready, ctx_done,
         ctxn_ready, ct_done, cts_ready, attn_done, h1_ready, stats2_done, moments2, var2_ready,
         rstd2_ready, n2_ready, hb2_ready, n2t_done, n2hi_ready, n2lo_ready,
         zeroed, masks_ready, abs_part, abs_ready, abs_total, limit_ready, neg_limit_ready, cmp_done,
         tern_ready, up_done, gelu_done, hi_done, lo_done, down_done, y_ready, y_stored0,
         y_stored1) = s.values()
        y_stored = [y_stored0, y_stored1]
        closed_off, expo_ready, v_cleared, kxa_ready = (sem(n) for n in ("closed_off", "expo_ready", "v_cleared", "kxa_ready"))

        LEAD, LAG = 2, 2

        def live(j):
            return not isinstance(j, int) or 0 <= j < NC

        def upto(j, per=1):
            return per * j + per

        def lone(eng):
            eng.wait_ge(idx_landed, 16).then_inc(closed_off, 1)

        def tile(j, t):
            return bass.ds((j * T + t) * E, E)

        def chunk(j):
            return bass.ds(j * (T * E), T * E)

        block = ctx.enter_context(nc.Block())

        @block.sync
        def _(sp):
            sp.dma_start(idx_sb[:], idx).then_inc(idx_landed, 16)
            sp.dma_start(bias_rows[:], rows).then_inc(rows_landed_dma, 16)
            sp.dma_start(wk_sb[:], wk).then_inc(wqk_landed, 16)
            sp.dma_start(wq_sb[:], wq).then_inc(wqk_landed, 16)

            def count_gathers(chunks):
                for c in chunks:
                    sp.wait_ge(gathered[c], 16 * T).then_inc(emb_landed, 1)

            count_gathers(range(2))
            sp.dma_start(wv_sb[:], wv).then_inc(wvo_landed, 16)
            sp.dma_start(wo_sb[:], wo).then_inc(wvo_landed, 16)
            sp.dma_start(w1_sb[:], w1).then_inc(wff_landed, 16)
            sp.dma_start(w2_sb[:], w2).then_inc(wff_landed, 16)
            count_gathers(range(2, NC))
            out_v = out.rearrange("(m t p) e -> m p t e", t=BT, p=P)

            def store(i, b, m):
                sp.wait_ge(y_ready, upto(m))
                lone(sp)
                sp.dma_start(out_v[bass.ds(m, 1)].rearrange("o p t e -> p (o t) e"), y[:, b]).then_inc(y_stored[b], 16)

            with sp.Fori(0, NB // 2) as i:
                for b in range(2):
                    store(i, b, 2 * i + b)
            for b in range(2):
                sp.wait_ge(y_stored[b], 16 * (NB // 2))

        @block.gpsimd
        def _(pool):
            pool.wait_ge(idx_landed, 16)

            def gather(c):
                for t in range(T * c, T * c + T):
                    nc.gpsimd.indirect_dma_start(
                        hid[:, t * E:(t + 1) * E], None, table,
                        bass.IndirectOffsetOnAxis(ap=idx_sb[:, t:t + 1], axis=0),
                    ).then_inc(gathered[c], 16)

            def add_row(j, row):
                return nc.gpsimd.tensor_tensor(hid[:, chunk(j)], hid[:, chunk(j)], bias_rows[:, row, :], ALU.add)

            def inverse_deviation(mom, var, rstd, var_ready, rstd_ready, j):
                nc.gpsimd.tensor_scalar(var[:], mom[:, :, 1], EPS, None, ALU.add).then_inc(var_ready, 1)
                pool.wait_ge(var_ready, upto(j))
                lone(pool)
                nc.gpsimd.tensor_tensor(rstd[:], var[:], expo[:], ALU.pow).then_inc(rstd_ready, 1)

            def step(c):
                if live(c + 2):
                    pool.wait_ge(moments1, upto(c + 2))
                    if live(c + 1):
                        pool.wait_ge(n1_ready, upto(c + 1))
                    lone(pool)
                    inverse_deviation(mom1, var1, rstd1, var1_ready, rstd1_ready, c + 2)
                if live(c - 1):
                    pool.wait_ge(moments2, upto(c - 1))
                    if live(c - 2):
                        pool.wait_ge(n2_ready, upto(c - 2))
                    lone(pool)
                    inverse_deviation(mom2, var2, rstd2, var2_ready, rstd2_ready, c - 1)
                if live(c + 3):
                    pool.wait_ge(emb_landed, upto(c + 3))
                    lone(pool)
                    add_row(c + 3, ROW_TOK).then_inc(h_biased, 1)
                if live(c + 2):
                    pool.wait_ge(n1_ready, upto(c + 2))
                    lone(pool)
                    add_row(c + 2, ROW_BO).then_inc(hbo_ready, 1)
                if live(c - 1):
                    pool.wait_ge(n2_ready, upto(c - 1))
                    lone(pool)
                    add_row(c - 1, ROW_B2).then_inc(hb2_ready, 1)
                if live(c - 1):
                    pool.wait_ge(cmp_done, upto(c - 1))
                    lone(pool)
                    for w, dst in enumerate((t1, t2)):
                        last = nc.gpsimd.tensor_tensor(dst[:, bass.ds((c - 1) * P, P)], above[:, w, :], below[:, w, :],
                                                       ALU.subtract)
                    last.then_inc(tern_ready, 1)

            gather(0)
            gather(1)
            nc.gpsimd.memset(expo[:], -0.5).then_inc(expo_ready, 1)
            pool.wait_ge(expo_ready, 1)
            pool.wait_ge(rows_landed_dma, 16)
            pool.wait_ge(emb_landed, 1)
            add_row(0, ROW_TOK).then_inc(h_biased, 1)
            gather(2)
            step(-2)
            step(-1)
            for c, more in ((0, range(3, 7)), (1, range(7, 11)), (2, range(11, 14)), (3, range(14, NC))):
                for k in more:
                    gather(k)
                step(c)
            with pool.Fori(4, NC - 3) as c:
                step(c)
            for c in range(NC - 3, NC + LAG):
                step(c)

        @block.vector
        def _(dve):
            def moments(stats, mom, done):
                for t in range(T):
                    last = nc.vector.bn_aggr(mom[:, t, :], stats[:, t, :])
                last.then_inc(done, 1)

            def normalise(n, mom, rstd, j, ready):
                for t in range(T):
                    last = nc.vector.tensor_scalar(n[:, t, :], hid[:, tile(j, t)], mom[:, t, 0:1],
                                                   rstd[:, t:t + 1], ALU.subtract, ALU.mult)
                last.then_inc(ready, 1)

            def step(c):
                if live(c - 2):
                    dve.wait_ge(n2hi_ready, upto(c - 2))
                    at = bass.ds((c - 2) * CT, CT)
                    nc.vector.tensor_tensor(n2_lo[:, :, at], ps_on.rearrange("p (k n) -> p k n", k=KT),
                                            n2_hi[:, :, at], ALU.subtract).then_inc(n2lo_ready, 1)
                if live(c):
                    if live(c - 1):
                        dve.wait_ge(shift_done, upto(c - 1, T))
                    for t in range(T):
                        dve.wait_ge(scores_done, c * T + t + 1)
                        nc.vector.tensor_reduce(row_max[:, t, :], ps_scores[t].rearrange("p (h k) -> p h k", k=32),
                                                X, ALU.max).then_inc(max_done, 1)
                    for t in range(T):
                        if live(c - 1):
                            dve.wait_ge(exp_done, (c - 1) * T + t + 1)
                        dve.wait_ge(max_done, c * T + t + 1)
                        nc.vector.tensor_tensor(shifted[:, t, :].rearrange("p (h k) -> p h k", k=32),
                                                ps_scores[t].rearrange("p (h k) -> p h k", k=32),
                                                row_max[:, t, :].unsqueeze(2).to_broadcast([P, NH, 32]),
                                                ALU.subtract).then_inc(shift_done, 1)
                if live(c + 2):
                    dve.wait_ge(h_biased, upto(c + 2))
                    if live(c + 1):
                        dve.wait_ge(moments1, upto(c + 1))
                    lone(dve)
                    for t in range(T):
                        last = nc.vector.bn_stats(stats1[:, t, :], hid[:, tile(c + 2, t)])
                    last.then_inc(stats1_done, 1)
                    dve.wait_ge(stats1_done, upto(c + 2))
                    if live(c + 1):
                        dve.wait_ge(n1_ready, upto(c + 1))
                        dve.wait_ge(rstd1_ready, upto(c + 1))
                    lone(dve)
                    moments(stats1, mom1, moments1)
                if live(c - 1):
                    dve.wait_ge(hbo_ready, upto(c - 1))
                    dve.wait_ge(attn_done, upto(c - 1))
                    nc.vector.tensor_tensor(hid[:, chunk(c - 1)], ps_on, hid[:, chunk(c - 1)], ALU.add)\
                        .then_inc(h1_ready, 1)
                    dve.wait_ge(h1_ready, upto(c - 1))
                    if live(c - 2):
                        dve.wait_ge(moments2, upto(c - 2))
                    lone(dve)
                    for t in range(T):
                        last = nc.vector.bn_stats(stats2[:, t, :], hid[:, tile(c - 1, t)])
                    last.then_inc(stats2_done, 1)
                    dve.wait_ge(stats2_done, upto(c - 1))
                    if live(c - 2):
                        dve.wait_ge(n2_ready, upto(c - 2))
                        dve.wait_ge(rstd2_ready, upto(c - 2))
                    lone(dve)
                    moments(stats2, mom2, moments2)
                if live(c + 2):
                    dve.wait_ge(rstd1_ready, upto(c + 2))
                    if live(c + 1):
                        dve.wait_ge(nt_done, upto(c + 1))
                    normalise(n1, mom1, rstd1, c + 2, n1_ready)
                if live(c - 1):
                    if not isinstance(c, int) or c >= 2:
                        dve.wait_ge(tern_ready, upto(c - 2))
                    for w, src in enumerate((w1_sb, w2_sb)):
                        part = src[:, bass.ds((c - 1) * P, P)]
                        nc.vector.tensor_scalar(above[:, w, :], part, limit[:, w:w + 1], None, ALU.is_gt)
                        last = nc.vector.tensor_scalar(below[:, w, :], part, neg_limit[:, w:w + 1], None, ALU.is_lt)
                    last.then_inc(cmp_done, 1)
                if live(c - 1):
                    dve.wait_ge(rstd2_ready, upto(c - 1))
                    if live(c - 2):
                        dve.wait_ge(n2t_done, upto(c - 2))
                    normalise(n2, mom2, rstd2, c - 1, n2_ready)
                if live(c + 1):
                    dve.wait_ge(ks_ready, upto(c + 1))
                    if live(c):
                        dve.wait_ge(scores_done, upto(c, T))
                    for j in range(KX_ACT, HG):
                        last = nc.vector.tensor_scalar(k_x[:, :, j, :], k_t[:],
                                                       cols_sb[:, COL_HEAD + j:COL_HEAD + j + 1], None, ALU.mult)
                    last.then_inc(kx_ready, 1)
                if live(c):
                    dve.wait_ge(ctx_done, upto(c))
                    if live(c - 1):
                        dve.wait_ge(ctxn_ready, upto(c - 1))
                    nc.vector.reciprocal(row_inv[:], ps_ctx[:, :, :, HD]).then_inc(inv_done, 1)
                    dve.wait_ge(inv_done, upto(c))
                    if live(c - 1):
                        dve.wait_ge(ct_done, upto(c - 1))
                    nc.vector.tensor_tensor(ctx_n[:].rearrange("p t (h d) -> p t h d", d=HD), ps_ctx[:, :, :, 0:HD],
                                            row_inv[:].unsqueeze(3).to_broadcast([P, T, NH, HD]),
                                            ALU.mult).then_inc(ctxn_ready, 1)

            nc.vector.memset(v_x[:], 0.0).then_inc(v_cleared, 1)
            nc.vector.memset(ones[:], 1.0)
            dve.wait_ge(v_cleared, 1)
            for a in range(HQ):
                own = v_x[32 * a:32 * a + 32, :, :, a, :].rearrange("p t g (a d) -> p t g a d", d=HD + 1)
                for t in range(T):
                    last = nc.vector.memset(own[:, t, :, :, HD], 1.0)
            last.then_inc(zeroed, 1)
            dve.wait_ge(const_landed, 48)
            nc.vector.tensor_copy(ml_bf[:], ml_sb[:])
            nc.vector.tensor_copy(mr_bf[:], mr_sb[:]).then_inc(masks_ready, 1)
            dve.wait_ge(cols_landed, 16)
            dve.wait_ge(idx_landed, 16)
            step(-2)
            step(-1)
            dve.wait_ge(wff_landed, 32)
            for w, src in enumerate((w1_sb, w2_sb)):
                nc.vector.tensor_reduce(part_sum[:, w, :], src[:].rearrange("p (a n) -> p a n", a=16), X, ALU.add,
                                        apply_absolute_value=True).then_inc(abs_part, 1)
            dve.wait_ge(abs_part, 2)
            nc.vector.tensor_reduce(abs_sum[:], part_sum[:], X, ALU.add).then_inc(abs_ready, 1)
            step(0)
            dve.wait_ge(abs_total, 1)
            nc.vector.tensor_scalar(limit[:], ps_v[:, 0:2], 1.0 / (FF * E), 1e-8, ALU.mult, ALU.max)\
                .then_inc(limit_ready, 1)
            dve.wait_ge(limit_ready, 1)
            nc.vector.tensor_scalar(neg_limit[:], limit[:], -0.5, None, ALU.mult).then_inc(limit_ready, 1)
            dve.wait_ge(limit_ready, 2)
            nc.vector.tensor_scalar(limit[:], limit[:], 0.5, None, ALU.mult).then_inc(neg_limit_ready, 1)
            dve.wait_ge(neg_limit_ready, 1)
            step(1)
            with dve.Fori(LAG, NC - LEAD) as c:
                step(c)
            for c in range(NC - LEAD, NC + 1):
                step(c)

            def parts(b, m, f):
                slot = f % 2
                n = m * FB + f + 1
                dve.wait_ge(gelu_done, n)
                if not isinstance(m, int) or m >= 2:
                    dve.wait_ge(down_done, (m - 1) * BT)
                nc.vector.tensor_copy(act_hi[:, b, f, :], act[:, slot, :]).then_inc(hi_done, 1)
                dve.wait_ge(hi_done, n)
                nc.vector.tensor_tensor(act_lo[:, b, f, :], act[:, slot, :], act_hi[:, b, f, :], ALU.subtract)\
                    .then_inc(lo_done, 1)

            def finish(b, m, t):
                dve.wait_ge(down_done, m * BT + t + 1)
                if (not isinstance(m, int) or m >= 2) and t == 0:
                    dve.wait_ge(y_stored[b], 8 * (m - b))
                last = nc.vector.tensor_tensor(y[:, b, t, :], ps[:, 4 + t, 0:E],
                                               hid[:, bass.ds((m * BT + t) * E, E)], ALU.add)
                if t == BT - 1:
                    last.then_inc(y_ready, 1)

            def block_step(b, m):
                for f in range(FB):
                    parts(b, m, f)
                    if f % 2 == 1 and (not isinstance(m, int) or m >= 1):
                        finish(1 - b, m - 1, f // 2)

            block_step(0, 0)
            step(NC + 1)
            dve.wait_ge(hb2_ready, NC)
            block_step(1, 1)
            with dve.Fori(1, NB // 2) as i:
                for b in range(2):
                    block_step(b, 2 * i + b)
            for t in range(BT):
                finish(1, NB - 1, t)

        @block.scalar
        def _(act_e):
            act_e.dma_start(id_sb[:], ident).then_inc(const_landed, 16)
            act_e.dma_start(ml_sb[:], mask_l).then_inc(const_landed, 16)
            act_e.dma_start(mr_sb[:], mask_r).then_inc(const_landed, 16)
            act_e.dma_start(cols_sb[:], cols).then_inc(cols_landed, 16)
            act_e.wait_ge(idx_landed, 16)
            act_e.wait_ge(cols_landed, 16)

            def with_bias(dst, src, col, ready):
                for g in range(KT):
                    last = nc.scalar.activation(dst[:, g, :], src[:, g * CT:(g + 1) * CT], ACT.Identity,
                                                bias=cols_sb[:, col + g:col + g + 1])
                last.then_inc(ready, 1)

            def exps(c, t):
                act_e.wait_ge(shift_done, c * T + t + 1)
                if live(c - 1):
                    act_e.wait_ge(pt_done, (c - 1) * T + t + 1)
                nc.scalar.activation(prob[:, t, :], shifted[:, t, :], ACT.Exp, scale=SCALE).then_inc(exp_done, 1)

            def step(c):
                if live(c):
                    exps(c, 0)
                if live(c):
                    exps(c, 1)
                if live(c + 1):
                    act_e.wait_ge(k_done, upto(c + 1))
                    if live(c):
                        act_e.wait_ge(kx_ready, upto(c))
                        act_e.wait_ge(kxa_ready, upto(c))
                    with_bias(k_t, ps_k, COL_BK, ks_ready)
                    act_e.wait_ge(q_done, upto(c + 1))
                    if live(c):
                        act_e.wait_ge(scores_done, upto(c, T))
                    with_bias(q_t, ps_q, COL_BQ, qs_ready)
                if live(c):
                    for t in range(T):
                        act_e.wait_ge(pt_done, c * T + t + 1)
                        if live(c - 1):
                            act_e.wait_ge(ctx_done, upto(c - 1))
                        nc.scalar.activation(prob_t[:, t, :], ps_pt[t], ACT.Copy).then_inc(pts_ready, 1)
                if live(c + 1):
                    act_e.wait_ge(ks_ready, upto(c + 1))
                    for j in range(KX_ACT):
                        last = nc.scalar.activation(k_x[:, :, j, :], k_t[:], ACT.Copy,
                                                    scale=cols_sb[:, COL_HEAD + j:COL_HEAD + j + 1])
                    last.then_inc(kxa_ready, 1)
                if live(c + 2):
                    act_e.wait_ge(nt_done, upto(c + 2))
                    if live(c + 1):
                        act_e.wait_ge(v_done, upto(c + 1))
                    nc.scalar.activation(n1_t[:].rearrange("p k n -> p (k n)"), ps_nt, ACT.Copy)\
                        .then_inc(nts_ready, 1)
                if live(c):
                    act_e.wait_ge(ct_done, upto(c))
                    if live(c - 1):
                        act_e.wait_ge(attn_done, upto(c - 1))
                    with_bias(ctx_t, ps_ct, COL_BV, cts_ready)
                if live(c - 1):
                    act_e.wait_ge(n2t_done, upto(c - 1))
                    lone(act_e)
                    nc.scalar.activation(n2_hi[:, :, bass.ds((c - 1) * CT, CT)],
                                         ps_on.rearrange("p (k n) -> p k n", k=KT), ACT.Copy)\
                        .then_inc(n2hi_ready, 1)
                if live(c + 1):
                    act_e.wait_ge(v_done, upto(c + 1))
                    if live(c):
                        act_e.wait_ge(ctx_done, upto(c))
                    for g in range(G):
                        for a in range(HQ):
                            src = ps_v[32 * g:32 * g + 32, :].rearrange("p (t a q d) -> p t a q d", t=T, a=HQ, d=HD)
                            dst = v_x[32 * a:32 * a + 32, :, g, a, :].rearrange("p t (q d) -> p t q d", d=HD + 1)
                            last = nc.scalar.activation(dst[:, :, :, 0:HD], src[:, :, a], ACT.Copy)
                    last.then_inc(vx_ready, 1)

            act_e.wait_ge(zeroed, 1)
            nc.scalar.activation(warm[:], ones[:, 0:1], ACT.Exp)
            for c in range(-LEAD, LAG):
                step(c)
            with act_e.Fori(LAG, NC - LEAD) as c:
                step(c)
            for c in range(NC - LEAD, NC):
                step(c)

            def block_step(b, m):
                for f in range(FB):
                    slot = f % 2
                    n = m * FB + f + 1
                    act_e.wait_ge(up_done, n)
                    if (not isinstance(m, int) or m >= 1) or f >= 2:
                        act_e.wait_ge(lo_done, n - 2)
                    nc.scalar.activation(act[:, slot, :], ps[:, f % 4, :], ACT.Gelu,
                                         bias=cols_sb[:, COL_B1 + f:COL_B1 + f + 1]).then_inc(gelu_done, 1)

            block_step(0, 0)
            step(NC)
            block_step(1, 1)
            with act_e.Fori(1, NB // 2) as i:
                for b in range(2):
                    block_step(b, 2 * i + b)

        @block.tensor
        def _(pe):
            def mm(o, l, r, start, stop, **kw):
                return nc.tensor.matmul(o, l, r, start=start, stop=stop, **kw)

            def scores(c, t):
                pe.wait_ge(kx_ready, upto(c))
                pe.wait_ge(kxa_ready, upto(c))
                pe.wait_ge(qs_ready, upto(c))
                if live(c - 1):
                    pe.wait_ge(ctxn_ready, upto(c - 1))
                mm(ps_scores[t], ml_bf[:], mr_bf[:], True, False)
                for k in range(KT):
                    for g in range(G):
                        at = slice(t * P + 32 * g, t * P + 32 * g + 32)
                        last = mm(ps_scores[t][32 * g:32 * g + 32, k * 256:(k + 1) * 256]
                                  .rearrange("p (h n) -> p h n", h=HG),
                                  q_t[:, k, at], k_x[:, k, :, at], False, k == KT - 1)
                last.then_inc(scores_done, 1)

            def attn_out(j):
                pe.wait_ge(cts_ready, upto(j))
                if live(j - 1):
                    pe.wait_ge(n2lo_ready, upto(j - 1))
                for t in range(T):
                    for k in range(KT):
                        last = mm(ps_on[:, t * E:(t + 1) * E], ctx_t[:, k, t * P:(t + 1) * P], wo_sb[:, k, :],
                                  k == 0, k == KT - 1)
                last.then_inc(attn_done, 1)

            def transposes(dst, src):
                for k in range(KT):
                    for t in range(T):
                        last = nc.tensor.transpose(dst[:, k * CT + t * P:k * CT + (t + 1) * P],
                                                   src[:, t, k * P:(k + 1) * P], id_sb[:])
                return last

            def project(dst, w):
                for g in range(KT):
                    for k in range(KT):
                        last = mm(dst[:, g * CT:(g + 1) * CT], w[:, k, g * P:(g + 1) * P], n1_t[:, k, :],
                                  k == 0, k == KT - 1)
                return last

            def step(c, meanwhile=None):
                if live(c):
                    for t in range(T):
                        scores(c, t)
                if live(c - 1):
                    attn_out(c - 1)
                if live(c + 1):
                    pe.wait_ge(nts_ready, upto(c + 1))
                    project(ps_k, wk_sb).then_inc(k_done, 1)
                    project(ps_q, wq_sb).then_inc(q_done, 1)
                if live(c):
                    for t in range(T):
                        pe.wait_ge(exp_done, c * T + t + 1)
                        if live(c + 1):
                            pe.wait_ge([ks_ready, nts_ready][t], upto(c + 1))
                        for a in range(SW // P):
                            last = nc.tensor.transpose(ps_pt[t][:, a * P:(a + 1) * P],
                                                       prob[:, t, a * P:(a + 1) * P], id_sb[:])
                        last.then_inc(pt_done, 1)
                    pe.wait_ge(vx_ready, upto(c))
                    for t in range(T):
                        pe.wait_ge(pts_ready, c * T + t + 1)
                        for a in range(SW // P):
                            for g in range(G):
                                last = mm(ps_ctx[32 * g:32 * g + 32, t, a * HQ:(a + 1) * HQ, :],
                                          prob_t[:, t, a * P + 32 * g:a * P + 32 * g + 32],
                                          v_x[:, t, g, :, a * (HD + 1):(a + 1) * (HD + 1)], True, True)
                    last.then_inc(ctx_done, 1)
                if live(c + 1):
                    if live(c):
                        pe.wait_ge(vx_ready, upto(c))
                    for t in range(T):
                        for k in range(KT):
                            last = mm(ps_v[:, t * E:(t + 1) * E], n1_t[:, k, t * P:(t + 1) * P], wv_sb[:, k, :],
                                      k == 0, k == KT - 1)
                    last.then_inc(v_done, 1)
                if live(c + 2):
                    pe.wait_ge(n1_ready, upto(c + 2))
                    if live(c):
                        pe.wait_ge(pts_ready, upto(c, T))
                    transposes(ps_nt, n1).then_inc(nt_done, 1)
                if live(c):
                    pe.wait_ge(ctxn_ready, upto(c))
                    if live(c - 1):
                        pe.wait_ge(cts_ready, upto(c - 1))
                    transposes(ps_ct, ctx_n).then_inc(ct_done, 1)
                if meanwhile:
                    meanwhile()
                if live(c - 1):
                    pe.wait_ge(n2_ready, upto(c - 1))
                    transposes(ps_on, n2).then_inc(n2t_done, 1)

            pe.wait_ge(const_landed, 48)
            pe.wait_ge(masks_ready, 1)
            pe.wait_ge(zeroed, 1)
            step(-2)
            pe.wait_ge(wqk_landed, 32)
            pe.wait_ge(wvo_landed, 32)
            step(-1)
            step(0)
            pe.wait_ge(abs_ready, 1)
            pe.wait_ge(vx_ready, upto(1))
            mm(ps_v[:, 0:2], ones[:], abs_sum[:], True, True).then_inc(abs_total, 1)
            pe.wait_ge(limit_ready, 1)
            step(1)
            with pe.Fori(LAG, NC - LEAD) as c:
                step(c)
            for c in range(NC - LEAD, NC):
                step(c)


            def up(m, f):
                n = m * FB + f + 1
                if (not isinstance(m, int) or m >= 1) or f >= 4:
                    pe.wait_ge(gelu_done, n - 4)
                at = bass.ds(m * BT * P, BT * P)
                for i, part in enumerate((n2_hi, n2_lo)):
                    for k in range(KT):
                        last = mm(ps[:, f % 4, :], t1[:, k * FF + f * P:k * FF + (f + 1) * P], part[:, k, at],
                                  i + k == 0, i + k == 2)
                last.then_inc(up_done, 1)

            def down(b, m, f, t, half):
                if half == 0:
                    if t == 0:
                        pe.wait_ge(lo_done, m * FB + FB)
                    if not isinstance(m, int) or m >= 1:
                        pe.wait_ge(y_ready, upto(m - 1))
                for f in range(half * FB // 2, (half + 1) * FB // 2):
                    for i, part in enumerate((act_hi, act_lo)):
                        last = mm(ps[:, 4 + t, 0:E], part[:, b, f, t * P:(t + 1) * P], t2[:, f * E:(f + 1) * E],
                                  f + i == 0, f == FB - 1 and i == 1)
                if half == 1:
                    last.then_inc(down_done, 1)

            def block_step(b, m):
                for f in range(FB):
                    up(m, f)
                    if not isinstance(m, int) or m >= 1:
                        down(1 - b, m - 1, f, f // 2, f % 2)

            def first_block():
                pe.wait_ge(tern_ready, NC)
                pe.wait_ge(n2lo_ready, upto(BT // T - 1))
                block_step(0, 0)

            step(NC, first_block)
            pe.wait_ge(n2lo_ready, NC)
            block_step(1, 1)
            with pe.Fori(1, NB // 2) as i:
                for b in range(2):
                    block_step(b, 2 * i + b)
            for f in range(FB):
                down(1, NB - 1, f, f // 2, f % 2)


def kernel(x, L0_tok_W, L0_tok_b, L0_attn_in_proj_weight, L0_attn_in_proj_bias, L0_attn_out_proj_weight,
           L0_attn_out_proj_bias, L0_ffn_W1, L0_ffn_b1, L0_ffn_W2, L0_ffn_b2):
    import concourse.bacc as bacc
    from concourse.bass_utils import run_bass_kernel_spmd

    arr = np.asarray
    cont = np.ascontiguousarray

    def contract(w):
        w = arr(w)
        return cont(w.reshape(w.shape[0] // P, P, w.shape[1]).transpose(1, 0, 2))

    def by_partition(v):
        return cont(arr(v).reshape(-1, P).T)

    idx = cont(arr(x).T.reshape(NC * T, P).T)
    w_in = arr(L0_attn_in_proj_weight).reshape(NH, 3, HD, E)
    b_in = arr(L0_attn_in_proj_bias).reshape(NH, 3, HD)
    w_v = w_in[:, 2].reshape(NH // HQ, HQ, HD, E).transpose(1, 0, 2, 3).reshape(E, E)
    head = (np.arange(P)[:, None] // HD == np.arange(HG)[None, :]).astype(np.float32)
    cols = cont(np.concatenate([by_partition(b_in[:, 0]), by_partition(b_in[:, 1]), by_partition(b_in[:, 2]),
                                by_partition(L0_ffn_b1), head], axis=1))
    rows = cont(np.broadcast_to(np.stack([np.concatenate([arr(b), arr(b)]) for b in
                                          (L0_tok_b, L0_attn_out_proj_bias, L0_ffn_b2)]), (P, 3, T * E)))
    entry = np.arange(P) // S % 2
    mask_l = cont((entry[None, :] == np.arange(2)[:, None]).astype(np.float32))
    mask_r = cont(np.where(np.arange(SW)[None, :] // S % 2 == np.arange(2)[:, None], 0.0, FAR).astype(np.float32))
    arrays = {
        "idx": idx,
        "table": cont(arr(L0_tok_W).T),
        "rows": rows,
        "cols": cols,
        "wq": contract(w_in[:, 0].reshape(E, E).T),
        "wk": contract(w_in[:, 1].reshape(E, E).T),
        "wv": contract(w_v.T),
        "wo": contract(arr(L0_attn_out_proj_weight).T),
        "w1": contract(arr(L0_ffn_W1).T).reshape(P, KT * FF),
        "w2": contract(arr(L0_ffn_W2).T).reshape(P, FB * E),
        "ident": np.eye(P, dtype=np.float32),
        "mask_l": mask_l,
        "mask_r": mask_r,
    }
    nc = bacc.Bacc("TRN2", target_bir_lowering=False, num_devices=1)
    aps = [nc.dram_tensor(f"in_{n}", a.shape, mybir.dt.from_np(a.dtype), kind="ExternalInput").ap()
           for n, a in arrays.items()]
    out = nc.dram_tensor("out", (TOK, E), F32, kind="ExternalOutput").ap()
    build(nc, *aps, out)
    r = run_bass_kernel_spmd(nc, [{f"in_{n}": a for n, a in arrays.items()}], core_ids=[0])
    return cont(r.results[0]["out"].reshape(B, S, E).transpose(1, 0, 2))
```

```python
import numpy as np
import concourse.bass as bass
from concourse import mybir
from contextlib import ExitStack

F32 = mybir.dt.float32
F16 = mybir.dt.float16
BF16 = mybir.dt.bfloat16
I32 = mybir.dt.int32
ALU = mybir.AluOpType
ACT = mybir.ActivationFunctionType
X = mybir.AxisListType.X

P = 128
S, B, E = 16, 256, 256
NH, HD = 16, 16
FF = 4 * E
VOCAB = 50257
KT = E // P
T = 2
CT = T * P
TOK = S * B
NC = TOK // CT
G = P // 32
HG = P // HD
HQ = 4
SW = NH * 32
FB = FF // P
BT = 4
NB = TOK // (BT * P)
SCALE = HD ** -0.5
EPS = 1e-5
KX_ACT, KX_ACT_0, KX_SECOND = 4, 3, 6
CTX_ONES = 2.0 ** 8
W_TOP = 2.0 ** 12
FIRST_SPLIT = 3
UP_BANKS = (4, 5, 2, 3, 0, 1, 2, 3)
WARMUP = 32
FAR = -1e30

COL_BQ, COL_BK, COL_BV, COL_B1, COL_HEAD = 0, 2, 4, 6, 14
N_COLS = COL_HEAD + HG
ROW_TOK, ROW_BO, ROW_B2 = 0, 1, 2


def build(nc, idx, table, rows, cols, wq, wk, wv, wo, w1, w2, ident, mask_l, mask_r, out):
    with ExitStack() as ctx:
        def sb(name, shape, dt=F32):
            return ctx.enter_context(nc.sbuf_tensor(name, shape, dt))

        def sem(name):
            return ctx.enter_context(nc.semaphore(name))

        idx_sb = sb("idx_sb", [P, NC * T], I32)
        hid = sb("hid", [P, NC * CT * E // P])
        bias_rows = sb("bias_rows", [P, 3, T * E])
        cols_sb = sb("cols_sb", [P, N_COLS])
        wq_sb = sb("wq_sb", [P, KT, E])
        wk_sb = sb("wk_sb", [P, KT, E])
        wv_sb = sb("wv_sb", [P, KT, E])
        wo_sb = sb("wo_sb", [P, KT, E])
        w_hi = sb("w_hi", [P, 4, KT, E], F16)
        w_lo = sb("w_lo", [P, 4, KT, E], F16)
        w_max = sb("w_max", [P, 6])
        o_down = sb("o_down", [P, 1])
        bv_up = sb("bv_up", [P, KT])
        w_spread = sb("w_spread", [P, P])
        w_up = sb("w_up", [P, 1])
        w_pow2 = sb("w_pow2", [P, 1])
        w_down = sb("w_down", [P, 1])
        w1_sb = sb("w1_sb", [P, KT * FF])
        w2_sb = sb("w2_sb", [P, FB * E])
        t1 = sb("t1", [P, KT * FF], BF16)
        t2 = sb("t2", [P, FB * E], BF16)
        id_sb = sb("id_sb", [P, P])
        ml_sb = sb("ml_sb", [2, P])
        mr_sb = sb("mr_sb", [2, SW])
        ml_bf = sb("ml_bf", [2, P], BF16)
        mr_bf = sb("mr_bf", [2, SW], BF16)
        ones = sb("ones", [P, P])
        warm = sb("warm", [P, 1])
        expo = sb("expo", [P, T])
        part_sum = sb("part_sum", [P, 2, 16])
        abs_sum = sb("abs_sum", [P, 2])
        limit = sb("limit", [P, 2])
        neg_limit = sb("neg_limit", [P, 2])
        above = sb("above", [P, 2, P])
        below = sb("below", [P, 2, P])
        stats1 = sb("stats1", [P, T, 6])
        stats2 = sb("stats2", [P, T, 6])
        mom1 = sb("mom1", [P, T, 2])
        mom2 = sb("mom2", [P, T, 2])
        var1 = sb("var1", [P, T])
        var2 = sb("var2", [P, T])
        rstd1 = sb("rstd1", [P, T])
        rstd2 = sb("rstd2", [P, T])
        n1 = sb("n1", [P, T, E])
        n2 = sb("n2", [P, T, E])
        n1_t = sb("n1_t", [P, KT, CT])
        n1_hi, n1_lo = (n1_t[:].bitcast(F16)[:, :, i * CT:(i + 1) * CT] for i in range(2))
        q_t = sb("q_t", [P, KT, CT])
        k_t = sb("k_t", [P, KT, CT])
        k_x = sb("k_x", [P, KT, HG, CT])
        v_x = sb("v_x", [P, T, G, HQ, NH // HQ * (HD + 1)])
        row_max = sb("row_max", [P, T, NH])
        shifted = sb("shifted", [P, T, SW])
        prob = sb("prob", [P, T, SW])
        row_inv = sb("row_inv", [P, T, NH])
        prob_t = sb("prob_t", [P, T, SW])
        ctx_n = sb("ctx_n", [P, T, E])
        ctx_t = sb("ctx_t", [P, KT, CT])
        ctx_hi, ctx_lo = (ctx_t[:].bitcast(F16)[:, :, i * CT:(i + 1) * CT] for i in range(2))
        n2_hi = sb("n2_hi", [P, KT, TOK], F16)
        n2_lo = sb("n2_lo", [P, KT, TOK], F16)
        act = sb("act", [P, 2, BT * P])
        act_hi = sb("act_hi", [P, 2, FB, BT * P], F16)
        act_lo = sb("act_lo", [P, 2, FB, BT * P], F16)
        y = v_x[:].rearrange("p t g a x -> p (t g a x)")[:, 0:2 * BT * E].rearrange("p (b t e) -> p b t e", b=2, t=BT)

        ps = ctx.enter_context(nc.psum_tensor("ps", [P, 8, 512], F32))
        ps_scores = [ps[:, 0, :], ps[:, 1, :]]
        ps_ctx = ps[:, 0:2, 0:NH * (HD + 1)].rearrange("p t (h d) -> p t h d", d=HD + 1)
        ps_nt = ps[:, 2, :]
        ps_k = ps[:, 3, :]
        ps_q = ps[:, 4, :]
        ps_pt = [ps_k, ps_nt]
        ps_v = ps[:, 5, :]
        ps_ct = ps[:, 6, :]
        ps_on = ps[:, 7, :]

        idx_landed, rows_landed_dma, cols_landed = sem("idx_landed"), sem("rows_dma"), sem("cols_landed")
        wqk_landed, wvo_landed, wff_landed, const_landed = (sem(n) for n in ("wqk", "wvo", "wff", "const"))
        gathered = [sem(f"gathered{c}") for c in range(NC)]
        names = """emb_landed h_biased stats1_done moments1 var1_ready rstd1_ready n1_ready hbo_ready nt_done nts_ready
            q_done qs_ready k_done ks_ready kx_ready v_done vx_ready scores_done max_done shift_done
            exp_done inv_done pt_done pts_ready ctx_done ctxn_ready ct_done cts_ready attn_done h1_ready
            stats2_done moments2 var2_ready rstd2_ready n2_ready hb2_ready n2t_done n2hi_ready
            n2lo_ready zeroed masks_ready abs_part abs_ready abs_total limit_ready neg_limit_ready
            cmp_done tern_ready n1lo_ready w_maxima w_max_ready w_spread_ready w_all w_top_ready
            w_pow2_ready w_up_ready w_down_ready o_down_ready bvup_ready ctxlo_ready w_hi_ready
            w_lo_ready up_done gelu_done hi_done lo_done down_done y_ready y_stored0 y_stored1"""
        (emb_landed, h_biased, stats1_done, moments1, var1_ready, rstd1_ready, n1_ready, hbo_ready, nt_done,
         nts_ready, q_done, qs_ready, k_done, ks_ready, kx_ready, v_done, vx_ready, scores_done, max_done,
         shift_done, exp_done, inv_done, pt_done, pts_ready, ctx_done, ctxn_ready, ct_done, cts_ready,
         attn_done, h1_ready, stats2_done, moments2, var2_ready, rstd2_ready, n2_ready, hb2_ready, n2t_done,
         n2hi_ready, n2lo_ready, zeroed, masks_ready, abs_part, abs_ready, abs_total, limit_ready,
         neg_limit_ready, cmp_done, tern_ready, n1lo_ready, w_maxima, w_max_ready, w_spread_ready, w_all,
         w_top_ready, w_pow2_ready, w_up_ready, w_down_ready, o_down_ready, bvup_ready, ctxlo_ready,
         w_hi_ready, w_lo_ready, up_done, gelu_done, hi_done, lo_done, down_done, y_ready, y_stored0,
         y_stored1) = (sem(n) for n in names.split())
        y_stored = [y_stored0, y_stored1]
        closed_off, expo_ready, v_cleared, kxa_ready, h_biased0 = (
            sem(n) for n in ("closed_off", "expo_ready", "v_cleared", "kxa_ready", "h_biased0"))
        ones_ready, ones_scaled = sem("ones_ready"), sem("ones_scaled")

        LEAD, LAG = 2, 2
        LOOP = FIRST_SPLIT + 1

        def live(j):
            return not isinstance(j, int) or 0 <= j < NC

        def split(j):
            return not isinstance(j, int) or j >= FIRST_SPLIT

        def kx_act(j):
            return KX_ACT_0 if isinstance(j, int) and j == 0 else KX_ACT

        def upto(j, per=1):
            return per * j + per

        def lone(eng):
            eng.wait_ge(idx_landed, 16).then_inc(closed_off, 1)

        def up_bank(m, f):
            return UP_BANKS[f] if isinstance(m, int) and m == 0 else f % 4

        def tile(j, t):
            return bass.ds((j * T + t) * E, E)

        def chunk(j):
            return bass.ds(j * (T * E), T * E)

        block = ctx.enter_context(nc.Block())

        @block.sync
        def _(sp):
            sp.dma_start(idx_sb[:], idx).then_inc(idx_landed, 16)
            sp.dma_start(bias_rows[:], rows).then_inc(rows_landed_dma, 16)
            sp.dma_start(wk_sb[:], wk).then_inc(wqk_landed, 16)
            sp.dma_start(wq_sb[:], wq).then_inc(wqk_landed, 16)

            def count_gathers(chunks):
                for c in chunks:
                    sp.wait_ge(gathered[c], 16 * T).then_inc(emb_landed, 1)

            count_gathers(range(2))
            sp.dma_start(wv_sb[:], wv).then_inc(wvo_landed, 16)
            sp.dma_start(wo_sb[:], wo).then_inc(wvo_landed, 16)
            sp.dma_start(w1_sb[:], w1).then_inc(wff_landed, 16)
            sp.dma_start(w2_sb[:], w2).then_inc(wff_landed, 16)
            count_gathers(range(2, NC))
            out_v = out.rearrange("(m t p) e -> m p t e", t=BT, p=P)

            def store(i, b, m):
                sp.wait_ge(y_ready, upto(m, BT))
                lone(sp)
                sp.dma_start(out_v[bass.ds(m, 1)].rearrange("o p t e -> p (o t) e"), y[:, b]).then_inc(y_stored[b], 16)

            with sp.Fori(0, NB // 2 - 1) as i:
                for b in range(2):
                    store(i, b, 2 * i + b)
            store(NB // 2 - 1, 0, NB - 2)
            for t in range(BT):
                sp.wait_ge(y_ready, (NB - 1) * BT + t + 1)
                sp.dma_start(out_v[NB - 1, :, t, :], y[:, 1, t, :]).then_inc(y_stored[1], 16)
            sp.wait_ge(y_stored[0], 16 * (NB // 2))
            sp.wait_ge(y_stored[1], 16 * (NB // 2 - 1 + BT))

        @block.gpsimd
        def _(pool):
            pool.wait_ge(idx_landed, 16)

            def gather(c):
                for t in range(T * c, T * c + T):
                    nc.gpsimd.indirect_dma_start(
                        hid[:, t * E:(t + 1) * E], None, table,
                        bass.IndirectOffsetOnAxis(ap=idx_sb[:, t:t + 1], axis=0),
                    ).then_inc(gathered[c], 16)

            def add_row(j, row):
                return nc.gpsimd.tensor_tensor(hid[:, chunk(j)], hid[:, chunk(j)], bias_rows[:, row, :], ALU.add)

            def inverse_deviation(mom, var, rstd, var_ready, rstd_ready, j):
                nc.gpsimd.tensor_scalar(var[:], mom[:, :, 1], EPS, None, ALU.add).then_inc(var_ready, 1)
                pool.wait_ge(var_ready, upto(j))
                lone(pool)
                nc.gpsimd.tensor_tensor(rstd[:], var[:], expo[:], ALU.pow).then_inc(rstd_ready, 1)

            def ternary(k):
                pool.wait_ge(cmp_done, k + 1)
                lone(pool)
                for w, dst in enumerate((t1, t2)):
                    last = nc.gpsimd.tensor_tensor(dst[:, bass.ds(k * P, P)], above[:, w, :], below[:, w, :],
                                                   ALU.subtract)
                last.then_inc(tern_ready, 1)

            def step(c, before_ternary=None):
                if live(c + 2):
                    pool.wait_ge(moments1, upto(c + 2))
                    if live(c + 1):
                        pool.wait_ge(n1_ready, upto(c + 1))
                    lone(pool)
                    inverse_deviation(mom1, var1, rstd1, var1_ready, rstd1_ready, c + 2)
                if live(c - 1):
                    pool.wait_ge(moments2, upto(c - 1))
                    if live(c - 2):
                        pool.wait_ge(n2_ready, upto(c - 2))
                    lone(pool)
                    inverse_deviation(mom2, var2, rstd2, var2_ready, rstd2_ready, c - 1)
                if live(c + 3) and not (isinstance(c, int) and c == -2):
                    pool.wait_ge(emb_landed, upto(c + 3))
                    lone(pool)
                    add_row(c + 3, ROW_TOK).then_inc(h_biased, 1)
                if live(c + 2):
                    pool.wait_ge(n1_ready, upto(c + 2))
                    lone(pool)
                    add_row(c + 2, ROW_BO).then_inc(hbo_ready, 1)
                if live(c - 1):
                    pool.wait_ge(n2_ready, upto(c - 1))
                    lone(pool)
                    add_row(c - 1, ROW_B2).then_inc(hb2_ready, 1)
                if before_ternary:
                    before_ternary()
                if not isinstance(c, int) or 1 <= c < NC - 1:
                    ternary(c + 1)

            gather(0)
            gather(1)
            nc.gpsimd.memset(expo[:], -0.5).then_inc(expo_ready, 1)
            gather(2)
            pool.wait_ge(expo_ready, 1)
            pool.wait_ge(rows_landed_dma, 16)
            step(-2)
            step(-1)
            def gathers(*chunks):
                for c in chunks:
                    gather(c)

            gathers(3, 4, 5, 6)
            step(0)
            gather(7)
            ternary(0)
            ternary(1)
            step(1, before_ternary=lambda: gather(8))
            gather(9)
            step(2, before_ternary=lambda: gather(10))
            gather(11)
            step(3, before_ternary=lambda: gather(12))
            gather(13)
            step(4, before_ternary=lambda: gather(14))
            gather(15)
            with pool.Fori(5, NC - 3) as c:
                step(c)
            for c in range(NC - 3, NC + LAG):
                step(c)

        @block.vector
        def _(dve):
            def moments(stats, mom, done):
                for t in range(T):
                    last = nc.vector.bn_aggr(mom[:, t, :], stats[:, t, :])
                last.then_inc(done, 1)

            def normalise(n, mom, rstd, j, ready):
                for t in range(T):
                    last = nc.vector.tensor_scalar(n[:, t, :], hid[:, tile(j, t)], mom[:, t, 0:1],
                                                   rstd[:, t:t + 1], ALU.subtract, ALU.mult)
                last.then_inc(ready, 1)

            def compare(k):
                if not isinstance(k, int) or k >= 1:
                    dve.wait_ge(tern_ready, k)
                for w, src in enumerate((w1_sb, w2_sb)):
                    part = src[:, bass.ds(k * P, P)]
                    nc.vector.tensor_scalar(above[:, w, :], part, limit[:, w:w + 1], None, ALU.is_gt)
                    last = nc.vector.tensor_scalar(below[:, w, :], part, neg_limit[:, w:w + 1], None, ALU.is_lt)
                last.then_inc(cmp_done, 1)

            def spread_keys(j, heads):
                if live(j):
                    dve.wait_ge(ks_ready, upto(j))
                    if live(j - 1):
                        dve.wait_ge(scores_done, upto(j - 1, T))
                    for h in heads:
                        last = nc.vector.tensor_scalar(k_x[:, :, h, :], k_t[:],
                                                       cols_sb[:, COL_HEAD + h:COL_HEAD + h + 1], None, ALU.mult)
                    last.then_inc(kx_ready, 1)

            def low_part(j):
                dve.wait_ge(n2hi_ready, upto(j))
                at = bass.ds(j * CT, CT)
                nc.vector.tensor_tensor(n2_lo[:, :, at], ps_on.rearrange("p (k n) -> p k n", k=KT),
                                        n2_hi[:, :, at], ALU.subtract).then_inc(n2lo_ready, 1)

            def step(c, before_residual=None, before_context=None, after_context=None,
                     before_n1_low=None, before_n2=None):
                if live(c):
                    if live(c - 1):
                        dve.wait_ge(shift_done, upto(c - 1, T))
                    for t in range(T):
                        dve.wait_ge(scores_done, c * T + t + 1)
                        nc.vector.tensor_reduce(row_max[:, t, :], ps_scores[t].rearrange("p (h k) -> p h k", k=32),
                                                X, ALU.max).then_inc(max_done, 1)
                    for t in range(T):
                        if live(c - 1):
                            dve.wait_ge(exp_done, (c - 1) * T + t + 1)
                        dve.wait_ge(max_done, c * T + t + 1)
                        nc.vector.tensor_tensor(shifted[:, t, :].rearrange("p (h k) -> p h k", k=32),
                                                ps_scores[t].rearrange("p (h k) -> p h k", k=32),
                                                row_max[:, t, :].unsqueeze(2).to_broadcast([P, NH, 32]),
                                                ALU.subtract).then_inc(shift_done, 1)
                if live(c + 2):
                    if isinstance(c, int) and c < 0:
                        dve.wait_ge(rows_landed_dma, 16)
                        dve.wait_ge(emb_landed, upto(c + 2))
                        nc.vector.tensor_tensor(hid[:, chunk(c + 2)], hid[:, chunk(c + 2)],
                                                bias_rows[:, ROW_TOK, :], ALU.add).then_inc(h_biased0, 1)
                        dve.wait_ge(h_biased0, upto(c + 2))
                    else:
                        dve.wait_ge(h_biased, upto(c + 2) - 2)
                    if live(c + 1):
                        dve.wait_ge(moments1, upto(c + 1))
                    lone(dve)
                    for t in range(T):
                        last = nc.vector.bn_stats(stats1[:, t, :], hid[:, tile(c + 2, t)])
                    last.then_inc(stats1_done, 1)
                if before_residual:
                    before_residual()
                if live(c - 1):
                    dve.wait_ge(hbo_ready, upto(c - 1))
                    dve.wait_ge(attn_done, upto(c - 1))
                    if split(c - 1):
                        lone(dve)
                        nc.vector.scalar_tensor_tensor(hid[:, chunk(c - 1)], ps_on, o_down[:], hid[:, chunk(c - 1)],
                                                       ALU.mult, ALU.add).then_inc(h1_ready, 1)
                    else:
                        nc.vector.tensor_tensor(hid[:, chunk(c - 1)], ps_on, hid[:, chunk(c - 1)], ALU.add)\
                            .then_inc(h1_ready, 1)
                if live(c + 2):
                    dve.wait_ge(stats1_done, upto(c + 2))
                    if live(c + 1):
                        dve.wait_ge(n1_ready, upto(c + 1))
                        dve.wait_ge(rstd1_ready, upto(c + 1))
                    lone(dve)
                    moments(stats1, mom1, moments1)
                if live(c - 1):
                    dve.wait_ge(h1_ready, upto(c - 1))
                    if live(c - 2):
                        dve.wait_ge(moments2, upto(c - 2))
                    lone(dve)
                    for t in range(T):
                        last = nc.vector.bn_stats(stats2[:, t, :], hid[:, tile(c - 1, t)])
                    last.then_inc(stats2_done, 1)
                first_heads = range(kx_act(c + 1), KX_SECOND)
                if not (isinstance(c, int) and c == -1):
                    spread_keys(c + 1, first_heads)
                if live(c - 1):
                    dve.wait_ge(stats2_done, upto(c - 1))
                    if live(c - 2):
                        dve.wait_ge(n2_ready, upto(c - 2))
                        dve.wait_ge(rstd2_ready, upto(c - 2))
                    lone(dve)
                    moments(stats2, mom2, moments2)
                if live(c + 2):
                    dve.wait_ge(rstd1_ready, upto(c + 2))
                    if live(c + 1):
                        dve.wait_ge(nt_done, upto(c + 1))
                    normalise(n1, mom1, rstd1, c + 2, n1_ready)
                if before_n2:
                    before_n2()
                if isinstance(c, int) and c == -1:
                    spread_keys(c + 1, first_heads)
                spread_keys(c + 1, range(KX_SECOND, HG))
                if live(c - 1):
                    dve.wait_ge(rstd2_ready, upto(c - 1))
                    if live(c - 2):
                        dve.wait_ge(n2t_done, upto(c - 2))
                    normalise(n2, mom2, rstd2, c - 1, n2_ready)
                if before_context:
                    before_context()
                if live(c):
                    dve.wait_ge(ctx_done, upto(c))
                    if live(c - 1):
                        dve.wait_ge(ctxn_ready, upto(c - 1))
                    nc.vector.reciprocal(row_inv[:], ps_ctx[:, :, :, HD]).then_inc(inv_done, 1)
                    dve.wait_ge(inv_done, upto(c))
                    if live(c - 1):
                        dve.wait_ge(ct_done, upto(c - 1))
                    nc.vector.tensor_tensor(ctx_n[:].rearrange("p t (h d) -> p t h d", d=HD), ps_ctx[:, :, :, 0:HD],
                                            row_inv[:].unsqueeze(3).to_broadcast([P, T, NH, HD]),
                                            ALU.mult).then_inc(ctxn_ready, 1)
                if after_context:
                    after_context()
                if not isinstance(c, int) or 1 <= c < NC - 1:
                    compare(c + 1)
                if before_n1_low:
                    before_n1_low()
                if live(c + 2) and split(c + 2):
                    dve.wait_ge(nts_ready, upto(c + 2))
                    dve.wait_ge(v_done, upto(c + 1))
                    nc.vector.tensor_tensor(n1_lo, ps_nt.rearrange("p (k n) -> p k n", k=KT), n1_hi, ALU.subtract)\
                        .then_inc(n1lo_ready, 1)
                if live(c - 1) and not (isinstance(c, int) and c == NC):
                    low_part(c - 1)
                if live(c) and split(c):
                    dve.wait_ge(cts_ready, upto(c))
                    dve.wait_ge(attn_done, upto(c - 1))
                    for g in range(KT):
                        last = nc.vector.scalar_tensor_tensor(ctx_lo[:, g, :], ps_ct[:, g * CT:(g + 1) * CT],
                                                              bv_up[:, g:g + 1], ctx_hi[:, g, :], ALU.add,
                                                              ALU.subtract)
                    last.then_inc(ctxlo_ready, 1)

            nc.vector.memset(ones[:], 1.0).then_inc(ones_ready, 1)
            nc.vector.memset(v_x[:], 0.0).then_inc(v_cleared, 1)
            dve.wait_ge(v_cleared, 1)
            for a in range(HQ):
                own = v_x[32 * a:32 * a + 32, :, :, a, :].rearrange("p t g (a d) -> p t g a d", d=HD + 1)
                for t in range(T):
                    last = nc.vector.memset(own[:, t, :, :, HD], 1.0)
            last.then_inc(zeroed, 1)
            dve.wait_ge(const_landed, 48)
            nc.vector.tensor_copy(ml_bf[:], ml_sb[:])
            nc.vector.tensor_copy(mr_bf[:], mr_sb[:]).then_inc(masks_ready, 1)
            dve.wait_ge(cols_landed, 16)
            dve.wait_ge(idx_landed, 16)
            step(-2)
            step(-1)
            dve.wait_ge(wff_landed, 32)
            for w, src in enumerate((w1_sb, w2_sb)):
                nc.vector.tensor_reduce(part_sum[:, w, :], src[:].rearrange("p (a n) -> p a n", a=16), X, ALU.add,
                                        apply_absolute_value=True).then_inc(abs_part, 1)
            dve.wait_ge(abs_part, 2)
            nc.vector.tensor_reduce(abs_sum[:], part_sum[:], X, ALU.add).then_inc(abs_ready, 1)
            step(0)
            dve.wait_ge(abs_total, 1)
            nc.vector.tensor_scalar(limit[:], ps_on[:, 0:2], 1.0 / (FF * E), 1e-8, ALU.mult, ALU.max)\
                .then_inc(limit_ready, 1)
            dve.wait_ge(limit_ready, 1)
            nc.vector.tensor_scalar(neg_limit[:], limit[:], -0.5, None, ALU.mult).then_inc(limit_ready, 1)
            dve.wait_ge(limit_ready, 2)
            nc.vector.tensor_scalar(limit[:], limit[:], 0.5, None, ALU.mult).then_inc(neg_limit_ready, 1)
            dve.wait_ge(neg_limit_ready, 1)
            compare(0)
            dve.wait_ge(wqk_landed, 32)
            dve.wait_ge(wvo_landed, 32)
            for i, w in enumerate((wk_sb, wq_sb, wv_sb, wo_sb)):
                nc.vector.tensor_reduce(w_max[:, i:i + 1], w[:].rearrange("p k n -> p (k n)"), X, ALU.max,
                                        apply_absolute_value=True).then_inc(w_maxima, 1)
            nc.vector.tensor_reduce(w_max[:, 4:5], cols_sb[:, COL_BV:COL_BV + KT], X, ALU.max,
                                    apply_absolute_value=True).then_inc(w_maxima, 1)
            dve.wait_ge(w_maxima, 5)
            nc.vector.tensor_reduce(w_max[:, 5:6], w_max[:, 0:5], X, ALU.max).then_inc(w_max_ready, 1)
            dve.wait_ge(w_max_ready, 1)
            nc.vector.tensor_scalar(w_spread[:], ones[:], w_max[:, 5:6], None, ALU.mult).then_inc(w_spread_ready, 1)
            compare(1)

            def weight_scale():
                dve.wait_ge(w_all, 1)
                nc.vector.tensor_reduce(w_pow2[:], ps_ct[:, 0:P], X, ALU.max).then_inc(w_top_ready, 1)
                dve.wait_ge(w_top_ready, 1)
                nc.vector.tensor_scalar(w_pow2[:], w_pow2[:], 1e-30, None, ALU.max).then_inc(w_top_ready, 1)
                dve.wait_ge(w_top_ready, 2)
                nc.vector.tensor_scalar(w_pow2[:].bitcast(I32), w_pow2[:].bitcast(I32), 0x7F800000, None,
                                        ALU.bitwise_and).then_inc(w_pow2_ready, 1)
                dve.wait_ge(w_pow2_ready, 1)
                nc.vector.tensor_scalar(w_down[:], w_pow2[:], 1 / W_TOP, None, ALU.mult).then_inc(w_down_ready, 1)
                dve.wait_ge(w_down_ready, 1)
                nc.vector.reciprocal(w_up[:], w_down[:]).then_inc(w_up_ready, 1)
                nc.vector.tensor_scalar(o_down[:], w_down[:], w_down[:], CTX_ONES, ALU.mult, ALU.mult)\
                    .then_inc(o_down_ready, 1)
                dve.wait_ge(w_up_ready, 1)
                nc.vector.tensor_scalar(bv_up[:], cols_sb[:, COL_BV:COL_BV + KT], w_up[:], 1 / CTX_ONES, ALU.mult,
                                        ALU.mult).then_inc(bvup_ready, 1)

            def low_weight(i):
                w = (wk_sb, wq_sb, wv_sb, wo_sb)[i]
                dve.wait_ge(w_up_ready, 1)
                dve.wait_ge(w_hi_ready, i + 1)
                nc.vector.scalar_tensor_tensor(w_lo[:, i], w[:], w_up[:], w_hi[:, i], ALU.mult, ALU.subtract)\
                    .then_inc(w_lo_ready, 1)

            def low_weights(*which):
                for i in which:
                    low_weight(i)

            step(1, before_residual=weight_scale, before_n1_low=lambda: low_weights(0, 1))

            def scale_ones():
                for a in range(HQ):
                    rows = slice(32 * a, 32 * a + 32)
                    own = v_x[rows, :, :, a, :].rearrange("p t g (a d) -> p t g a d", d=HD + 1)[:, :, :, :, HD]
                    last = nc.vector.tensor_scalar(own, own, CTX_ONES, None, ALU.mult)
                last.then_inc(ones_scaled, 1)

            step(2, before_residual=lambda: low_weights(2), after_context=scale_ones)
            step(3, before_context=lambda: low_weights(3))
            with dve.Fori(LOOP, NC - LEAD) as c:
                step(c)

            def parts(b, m, f):
                slot = f % 2
                n = m * FB + f + 1
                dve.wait_ge(gelu_done, n)
                if not isinstance(m, int) or m >= 2:
                    dve.wait_ge(down_done, (m - 1) * BT)
                nc.vector.tensor_copy(act_hi[:, b, f, :], act[:, slot, :]).then_inc(hi_done, 1)
                dve.wait_ge(hi_done, n)
                nc.vector.tensor_tensor(act_lo[:, b, f, :], act[:, slot, :], act_hi[:, b, f, :], ALU.subtract)\
                    .then_inc(lo_done, 1)

            def finish(b, m, t):
                dve.wait_ge(down_done, m * BT + t + 1)
                if (not isinstance(m, int) or m >= 2) and t == 0:
                    dve.wait_ge(y_stored[b], 8 * (m - b))
                nc.vector.tensor_tensor(y[:, b, t, :], ps[:, 4 + t, 0:E],
                                        hid[:, bass.ds((m * BT + t) * E, E)], ALU.add).then_inc(y_ready, 1)

            def block_step(b, m):
                for f in range(FB):
                    parts(b, m, f)
                    if f % 2 == 1:
                        finish(1 - b, m - 1, f // 2)
                    if isinstance(m, int) and m == 1 and f == 0:
                        low_part(NC - 1)
                        dve.wait_ge(hb2_ready, NC)

            def first_parts(*fs):
                for f in fs:
                    parts(0, 0, f)

            step(NC - 2)
            step(NC - 1, before_context=lambda: first_parts(0), after_context=lambda: first_parts(1, 2))
            step(NC, before_residual=lambda: first_parts(3, 4, 5), before_n2=lambda: first_parts(6, 7))
            block_step(1, 1)
            with dve.Fori(1, NB // 2) as i:
                for b in range(2):
                    block_step(b, 2 * i + b)
            for t in range(BT):
                finish(1, NB - 1, t)

        @block.scalar
        def _(act_e):
            act_e.dma_start(id_sb[:], ident).then_inc(const_landed, 16)
            act_e.dma_start(ml_sb[:], mask_l).then_inc(const_landed, 16)
            act_e.dma_start(mr_sb[:], mask_r).then_inc(const_landed, 16)
            act_e.dma_start(cols_sb[:], cols).then_inc(cols_landed, 16)
            act_e.wait_ge(idx_landed, 16)
            act_e.wait_ge(cols_landed, 16)

            def with_bias(dst, src, bias, col, ready, scale=1.0):
                for g in range(KT):
                    last = nc.scalar.activation(dst[:, g, :], src[:, g * CT:(g + 1) * CT], ACT.Identity,
                                                bias=bias[:, col + g:col + g + 1], scale=scale)
                last.then_inc(ready, 1)

            def unscale(j):
                return w_down[:] if split(j) else 1.0

            def exps(c, t):
                act_e.wait_ge(shift_done, c * T + t + 1)
                if live(c - 1):
                    act_e.wait_ge(pt_done, (c - 1) * T + t + 1)
                nc.scalar.activation(prob[:, t, :], shifted[:, t, :], ACT.Exp, scale=SCALE).then_inc(exp_done, 1)

            def high_part(j):
                act_e.wait_ge(n2t_done, upto(j))
                lone(act_e)
                nc.scalar.activation(n2_hi[:, :, bass.ds(j * CT, CT)],
                                     ps_on.rearrange("p (k n) -> p k n", k=KT), ACT.Copy)\
                    .then_inc(n2hi_ready, 1)

            def step(c, before_probs=None, before_n1=None, before_context=None):
                if live(c):
                    exps(c, 0)
                if live(c):
                    exps(c, 1)
                if live(c + 1):
                    act_e.wait_ge(k_done, upto(c + 1))
                    if live(c):
                        act_e.wait_ge(kx_ready, upto(c, 2))
                        act_e.wait_ge(kxa_ready, upto(c))
                    with_bias(k_t, ps_k, cols_sb, COL_BK, ks_ready, unscale(c + 1))
                    act_e.wait_ge(q_done, upto(c + 1))
                    if live(c):
                        act_e.wait_ge(scores_done, upto(c, T))
                    with_bias(q_t, ps_q, cols_sb, COL_BQ, qs_ready, unscale(c + 1))
                if before_probs:
                    before_probs()
                if live(c):
                    for t in range(T):
                        act_e.wait_ge(pt_done, c * T + t + 1)
                        if live(c - 1):
                            act_e.wait_ge(ctx_done, upto(c - 1))
                        nc.scalar.activation(prob_t[:, t, :], ps_pt[t], ACT.Copy).then_inc(pts_ready, 1)
                if live(c + 1):
                    act_e.wait_ge(ks_ready, upto(c + 1))
                    for j in range(kx_act(c + 1)):
                        last = nc.scalar.activation(k_x[:, :, j, :], k_t[:], ACT.Copy,
                                                    scale=cols_sb[:, COL_HEAD + j:COL_HEAD + j + 1])
                    last.then_inc(kxa_ready, 1)
                if before_n1:
                    before_n1()
                if live(c + 2):
                    act_e.wait_ge(nt_done, upto(c + 2))
                    if live(c + 1):
                        act_e.wait_ge(v_done, upto(c + 1))
                    nc.scalar.activation(n1_hi if split(c + 2) else n1_t[:],
                                         ps_nt.rearrange("p (k n) -> p k n", k=KT), ACT.Copy).then_inc(nts_ready, 1)
                if before_context:
                    before_context()
                if live(c - 1):
                    high_part(c - 1)
                if live(c):
                    act_e.wait_ge(ct_done, upto(c))
                    if live(c - 1):
                        act_e.wait_ge(attn_done, upto(c - 1))
                    if split(c):
                        with_bias(ctx_hi, ps_ct, bv_up, 0, cts_ready)
                    else:
                        with_bias(ctx_t, ps_ct, cols_sb, COL_BV, cts_ready)
                if live(c + 1):
                    act_e.wait_ge(v_done, upto(c + 1))
                    if live(c):
                        act_e.wait_ge(ctx_done, upto(c))
                    for g in range(G):
                        for a in range(HQ):
                            src = ps_v[32 * g:32 * g + 32, :].rearrange("p (t a q d) -> p t a q d", t=T, a=HQ, d=HD)
                            dst = v_x[32 * a:32 * a + 32, :, g, a, :].rearrange("p t (q d) -> p t q d", d=HD + 1)
                            last = nc.scalar.activation(dst[:, :, :, 0:HD], src[:, :, a], ACT.Copy)
                    last.then_inc(vx_ready, 1)

            act_e.wait_ge(zeroed, 1)
            nc.scalar.activation(warm[:], ones[:, 0:1], ACT.Exp)
            for c in range(-LEAD, 1):
                step(c)

            def high_weights(*which):
                act_e.wait_ge(w_up_ready, 1)
                for i in which:
                    w = (wk_sb, wq_sb, wv_sb, wo_sb)[i]
                    nc.scalar.activation(w_hi[:, i], w[:], ACT.Copy, scale=w_up[:]).then_inc(w_hi_ready, 1)

            step(1, before_n1=lambda: high_weights(0, 1, 2))
            act_e.wait_ge(w_down_ready, 1)
            act_e.wait_ge(bvup_ready, 1)
            step(2)
            high_weights(3)
            step(3)
            with act_e.Fori(LOOP, NC - LEAD) as c:
                step(c)

            def gelu(m, f):
                slot = f % 2
                n = m * FB + f + 1
                act_e.wait_ge(up_done, n)
                if (not isinstance(m, int) or m >= 1) or f >= 2:
                    act_e.wait_ge(lo_done, n - 2)
                nc.scalar.activation(act[:, slot, :], ps[:, up_bank(m, f), :], ACT.Gelu,
                                     bias=cols_sb[:, COL_B1 + f:COL_B1 + f + 1]).then_inc(gelu_done, 1)

            def gelus(m, *fs):
                for f in fs:
                    gelu(m, f)

            def block_step(b, m):
                gelus(m, *range(FB))

            step(NC - 2)
            step(NC - 1, before_probs=lambda: gelus(0, 0), before_context=lambda: gelus(0, 1, 2))
            gelus(0, 3, 4, 5, 6, 7)
            high_part(NC - 1)
            block_step(1, 1)
            with act_e.Fori(1, NB // 2) as i:
                for b in range(2):
                    block_step(b, 2 * i + b)

        @block.tensor
        def _(pe):
            def mm(o, l, r, start, stop, **kw):
                return nc.tensor.matmul(o, l, r, start=start, stop=stop, **kw)

            def scores(c, t):
                pe.wait_ge(kx_ready, upto(c, 2))
                pe.wait_ge(kxa_ready, upto(c))
                pe.wait_ge(qs_ready, upto(c))
                if live(c - 1):
                    pe.wait_ge(ctxn_ready, upto(c - 1))
                mm(ps_scores[t], ml_bf[:], mr_bf[:], True, False)
                for k in range(KT):
                    for g in range(G):
                        at = slice(t * P + 32 * g, t * P + 32 * g + 32)
                        last = mm(ps_scores[t][32 * g:32 * g + 32, k * 256:(k + 1) * 256]
                                  .rearrange("p (h n) -> p h n", h=HG),
                                  q_t[:, k, at], k_x[:, k, :, at], False, k == KT - 1)
                last.then_inc(scores_done, 1)

            def split_product(dst, pairs, i, t):
                for n, (w, x) in enumerate(pairs):
                    for k in range(KT):
                        last = mm(dst[:, t * E:(t + 1) * E], x[:, k, t * P:(t + 1) * P], w[:, i, k, :],
                                  n + k == 0, n + k == len(pairs) - 1 + KT - 1)
                return last

            def attn_out(j):
                pe.wait_ge(cts_ready, upto(j))
                if live(j - 1):
                    pe.wait_ge(n2lo_ready, upto(j - 1))
                if split(j):
                    pe.wait_ge(ctxlo_ready, upto(j) - FIRST_SPLIT)
                for t in range(T):
                    if split(j):
                        last = split_product(ps_on, ((w_hi, ctx_hi), (w_hi, ctx_lo), (w_lo, ctx_hi)), 3, t)
                    else:
                        for k in range(KT):
                            last = mm(ps_on[:, t * E:(t + 1) * E], ctx_t[:, k, t * P:(t + 1) * P], wo_sb[:, k, :],
                                      k == 0, k == KT - 1)
                last.then_inc(attn_done, 1)

            def transposes(dst, src):
                for k in range(KT):
                    for t in range(T):
                        last = nc.tensor.transpose(dst[:, k * CT + t * P:k * CT + (t + 1) * P],
                                                   src[:, t, k * P:(k + 1) * P], id_sb[:])
                return last

            part_pairs = ((w_hi, n1_hi), (w_hi, n1_lo), (w_lo, n1_hi))

            def split_weights(c, i):
                if isinstance(c, int) and c + 1 == FIRST_SPLIT:
                    pe.wait_ge(w_hi_ready, i + 1)
                    pe.wait_ge(w_lo_ready, i + 1)

            def project(j, dst, i):
                for g in range(KT):
                    if split(j):
                        for n, (w, x) in enumerate(part_pairs):
                            for k in range(KT):
                                last = mm(dst[:, g * CT:(g + 1) * CT], w[:, i, k, g * P:(g + 1) * P], x[:, k, :],
                                          n + k == 0, n + k == len(part_pairs) - 1 + KT - 1)
                    else:
                        for k in range(KT):
                            last = mm(dst[:, g * CT:(g + 1) * CT], (wk_sb, wq_sb)[i][:, k, g * P:(g + 1) * P],
                                      n1_t[:, k, :], k == 0, k == KT - 1)
                return last

            def values(j, t):
                if split(j):
                    last = split_product(ps_v, part_pairs, 2, t)
                else:
                    for k in range(KT):
                        last = mm(ps_v[:, t * E:(t + 1) * E], n1_t[:, k, t * P:(t + 1) * P], wv_sb[:, k, :],
                                  k == 0, k == KT - 1)
                return last

            def normalised(j):
                pe.wait_ge(n2_ready, upto(j))
                transposes(ps_on, n2).then_inc(n2t_done, 1)

            def step(c, before_output=None, during_softmax=None, before_context=None):
                if live(c):
                    for t in range(T):
                        scores(c, t)
                if before_output:
                    before_output()
                if live(c - 1):
                    attn_out(c - 1)
                if during_softmax:
                    during_softmax()
                if live(c + 1):
                    pe.wait_ge(nts_ready, upto(c + 1))
                    if split(c + 1):
                        pe.wait_ge(n1lo_ready, upto(c + 1) - FIRST_SPLIT)
                    for i, (dst, done) in enumerate(((ps_k, k_done), (ps_q, q_done))):
                        split_weights(c, i)
                        project(c + 1, dst, i).then_inc(done, 1)
                if live(c):
                    for t in range(T):
                        pe.wait_ge(exp_done, c * T + t + 1)
                        if live(c + 1):
                            pe.wait_ge([ks_ready, nts_ready][t], upto(c + 1))
                        for a in range(SW // P):
                            last = nc.tensor.transpose(ps_pt[t][:, a * P:(a + 1) * P],
                                                       prob[:, t, a * P:(a + 1) * P], id_sb[:])
                        last.then_inc(pt_done, 1)
                if live(c + 1):
                    if live(c):
                        pe.wait_ge(vx_ready, upto(c))
                    split_weights(c, 2)
                    values(c + 1, 0)
                if live(c):
                    pe.wait_ge(vx_ready, upto(c))
                    for t in range(T):
                        pe.wait_ge(pts_ready, c * T + t + 1)
                        for a in range(SW // P):
                            for g in range(G):
                                last = mm(ps_ctx[32 * g:32 * g + 32, t, a * HQ:(a + 1) * HQ, :],
                                          prob_t[:, t, a * P + 32 * g:a * P + 32 * g + 32],
                                          v_x[:, t, g, :, a * (HD + 1):(a + 1) * (HD + 1)], True, True)
                    last.then_inc(ctx_done, 1)
                if live(c + 1):
                    values(c + 1, 1).then_inc(v_done, 1)
                if live(c + 2):
                    pe.wait_ge(n1_ready, upto(c + 2))
                    if live(c):
                        pe.wait_ge(pts_ready, upto(c, T))
                    transposes(ps_nt, n1).then_inc(nt_done, 1)
                if before_context:
                    before_context()
                if live(c - 1) and not (isinstance(c, int) and c == NC):
                    normalised(c - 1)
                if live(c):
                    pe.wait_ge(ctxn_ready, upto(c))
                    if live(c - 1):
                        pe.wait_ge(cts_ready, upto(c - 1))
                        if split(c - 1):
                            pe.wait_ge(ctxlo_ready, upto(c - 1) - FIRST_SPLIT)
                    transposes(ps_ct, ctx_n).then_inc(ct_done, 1)

            pe.wait_ge(ones_ready, 1)
            pe.wait_ge(idx_landed, 16)
            for _ in range(WARMUP):
                mm(ps_ct[:, 0:P], ones[:], ones[:], True, True)
            pe.wait_ge(const_landed, 48)
            pe.wait_ge(masks_ready, 1)
            pe.wait_ge(zeroed, 1)
            step(-2)
            pe.wait_ge(wqk_landed, 32)
            pe.wait_ge(wvo_landed, 32)
            step(-1)

            def total_magnitudes():
                pe.wait_ge(abs_ready, 1)
                mm(ps_on[:, 0:2], ones[:], abs_sum[:], True, True).then_inc(abs_total, 1)

            step(0, before_context=total_magnitudes)
            pe.wait_ge(limit_ready, 1)

            def magnitudes():
                pe.wait_ge(w_spread_ready, 1)
                pe.wait_ge(cts_ready, 1)
                mm(ps_ct[:, 0:P], w_spread[:], id_sb[:], True, True).then_inc(w_all, 1)

            step(1, during_softmax=magnitudes, before_context=lambda: pe.wait_ge(w_top_ready, 1))
            step(2)
            pe.wait_ge(ones_scaled, 1)
            step(3)
            pe.wait_ge(w_hi_ready, 4)
            pe.wait_ge(w_lo_ready, 4)
            with pe.Fori(LOOP, NC - LEAD) as c:
                step(c)


            def up(m, f):
                n = m * FB + f + 1
                if (not isinstance(m, int) or m >= 1) or f >= 4:
                    pe.wait_ge(gelu_done, n - 4)
                at = bass.ds(m * BT * P, BT * P)
                for i, part in enumerate((n2_hi, n2_lo)):
                    for k in range(KT):
                        last = mm(ps[:, up_bank(m, f), :], t1[:, k * FF + f * P:k * FF + (f + 1) * P], part[:, k, at],
                                  i + k == 0, i + k == 2)
                last.then_inc(up_done, 1)

            def down(b, m, f, t, half):
                if half == 0 and (not isinstance(m, int) or m >= 1):
                    pe.wait_ge(y_ready, (m - 1) * BT + t + 1)
                for f in range(half * FB // 2, (half + 1) * FB // 2):
                    if t == 0:
                        pe.wait_ge(lo_done, m * FB + f + 1)
                    for i, part in enumerate((act_hi, act_lo)):
                        last = mm(ps[:, 4 + t, 0:E], part[:, b, f, t * P:(t + 1) * P], t2[:, f * E:(f + 1) * E],
                                  f + i == 0, f == FB - 1 and i == 1)
                if half == 1:
                    last.then_inc(down_done, 1)

            def block_step(b, m):
                for f in range(FB):
                    if isinstance(m, int) and m == 1 and f == 0:
                        up(1, 0)
                        up(1, 1)
                    elif not (isinstance(m, int) and m == 1 and f == 1):
                        up(m, f)
                    if isinstance(m, int) and m == 1 and f == 2:
                        normalised(NC - 1)
                    if isinstance(m, int) and m == 1 and f == 6:
                        pe.wait_ge(n2lo_ready, NC)
                    down(1 - b, m - 1, f, f // 2, f % 2)

            def ups(*fs):
                for f in fs:
                    if f == 0:
                        pe.wait_ge(tern_ready, NC)
                        pe.wait_ge(n2lo_ready, upto(BT // T - 1))
                    if f == 1:
                        pe.wait_ge(vx_ready, NC)
                    up(0, f)

            step(NC - 2)
            step(NC - 1, during_softmax=lambda: ups(0, 1), before_context=lambda: ups(2, 3))
            step(NC, before_output=lambda: ups(4, 5, 6))
            ups(7)
            block_step(1, 1)
            with pe.Fori(1, NB // 2) as i:
                for b in range(2):
                    block_step(b, 2 * i + b)
            for f in range(FB):
                down(1, NB - 1, f, f // 2, f % 2)


def kernel(x, L0_tok_W, L0_tok_b, L0_attn_in_proj_weight, L0_attn_in_proj_bias, L0_attn_out_proj_weight,
           L0_attn_out_proj_bias, L0_ffn_W1, L0_ffn_b1, L0_ffn_W2, L0_ffn_b2):
    import concourse.bacc as bacc
    from concourse.bass_utils import run_bass_kernel_spmd

    arr = np.asarray
    cont = np.ascontiguousarray

    def contract(w):
        w = arr(w)
        return cont(w.reshape(w.shape[0] // P, P, w.shape[1]).transpose(1, 0, 2))

    def by_partition(v):
        return cont(arr(v).reshape(-1, P).T)

    idx = cont(arr(x).T.reshape(NC * T, P).T)
    w_in = arr(L0_attn_in_proj_weight).reshape(NH, 3, HD, E)
    b_in = arr(L0_attn_in_proj_bias).reshape(NH, 3, HD)
    w_v = w_in[:, 2].reshape(NH // HQ, HQ, HD, E).transpose(1, 0, 2, 3).reshape(E, E)
    head = (np.arange(P)[:, None] // HD == np.arange(HG)[None, :]).astype(np.float32)
    cols = cont(np.concatenate([by_partition(b_in[:, 0]), by_partition(b_in[:, 1]), by_partition(b_in[:, 2]),
                                by_partition(L0_ffn_b1), head], axis=1))
    rows = cont(np.broadcast_to(np.stack([np.concatenate([arr(b), arr(b)]) for b in
                                          (L0_tok_b, L0_attn_out_proj_bias, L0_ffn_b2)]), (P, 3, T * E)))
    entry = np.arange(P) // S % 2
    mask_l = cont((entry[None, :] == np.arange(2)[:, None]).astype(np.float32))
    mask_r = cont(np.where(np.arange(SW)[None, :] // S % 2 == np.arange(2)[:, None], 0.0, FAR).astype(np.float32))
    arrays = {
        "idx": idx,
        "table": cont(arr(L0_tok_W).T),
        "rows": rows,
        "cols": cols,
        "wq": contract(w_in[:, 0].reshape(E, E).T),
        "wk": contract(w_in[:, 1].reshape(E, E).T),
        "wv": contract(w_v.T),
        "wo": contract(arr(L0_attn_out_proj_weight).T),
        "w1": contract(arr(L0_ffn_W1).T).reshape(P, KT * FF),
        "w2": contract(arr(L0_ffn_W2).T).reshape(P, FB * E),
        "ident": np.eye(P, dtype=np.float32),
        "mask_l": mask_l,
        "mask_r": mask_r,
    }
    nc = bacc.Bacc("TRN2", target_bir_lowering=False, num_devices=1)
    aps = [nc.dram_tensor(f"in_{n}", a.shape, mybir.dt.from_np(a.dtype), kind="ExternalInput").ap()
           for n, a in arrays.items()]
    out = nc.dram_tensor("out", (TOK, E), F32, kind="ExternalOutput").ap()
    build(nc, *aps, out)
    r = run_bass_kernel_spmd(nc, [{f"in_{n}": a for n, a in arrays.items()}], core_ids=[0])
    return cont(r.results[0]["out"].reshape(B, S, E).transpose(1, 0, 2))
```
